# Optimizing a Trainium2 kernel written in Bass

```python
import numpy as np
import jax
import jax.numpy as jnp

def _softmax(x, axis=-1):
    return jax.nn.softmax(x, axis=axis)

def _gelu(x):
    return jax.nn.gelu(x, approximate=True)

def _silu(x):
    return jax.nn.silu(x)

def _sigmoid(x):
    return jax.nn.sigmoid(x)

def _layernorm(x, axis=-1, eps=1e-05):
    m = jnp.mean(x, axis=axis, keepdims=True)
    v = jnp.var(x, axis=axis, keepdims=True)
    return (x - m) / jnp.sqrt(v + eps)

def _scatter_add(tgt, idx, src, axis=0):
    return tgt.at[idx].add(src)

def _segment_sum(src, seg, n):
    return jax.ops.segment_sum(src, seg, n)
kernel_name = 'mk_cond_resid_d4_seqx_r4_21c2b9'

def setup_inputs(seed: int=0):
    np.random.seed(seed)
    _w = jnp.asarray

    def _rec_inputs():
        import jax
        import jax.numpy as jnp
        _rk = jax.random.key(seed)
        x = 7.22e-05 + 1 * jax.random.normal(jax.random.fold_in(_rk, 1), (8, 256, 512), jnp.float32)
        _lenS = 256 - jax.random.randint(jax.random.fold_in(_rk, 7), (8,), 0, max(1, 256 // 4) + 1, jnp.int32)
        _lenS2 = 256 - jax.random.randint(jax.random.fold_in(_rk, 8), (8,), 0, max(1, 256 // 4) + 1, jnp.int32)
        cond_2048 = jax.random.bernoulli(jax.random.fold_in(_rk, 11), 0.5063, (8, 512)).astype(jnp.float32)
        return (x, cond_2048)
    x, cond_2048 = _rec_inputs()

    def _L0_cond_setup():
        import jax, jax.numpy as jnp
        import numpy as np
        NH = 8
        NEG = -1e+30
        key = jax.random.key(seed)
        k1, k2, k3, k4 = jax.random.split(key, 4)
        B, D, T = (4, 256, 512)
        x = jax.random.normal(k1, (B, D, T), dtype=jnp.float32)
        mask = jax.random.randint(k2, (B, T), 0, 2).astype(jnp.float32)
        lim = float(np.sqrt(6.0 / (D + D)))
        Wq = jax.random.uniform(k3, (D, D), dtype=jnp.float32, minval=-lim, maxval=lim)
        Wo = jax.random.uniform(k4, (D, D), dtype=jnp.float32, minval=-lim, maxval=lim)
        return {'x': x, 'mask': mask, 'Wq': Wq, 'Wo': Wo}
    _L0_cond_all = _L0_cond_setup()
    _L0_cond_in = {k: v for k, v in _L0_cond_all.items() if k in ('Wq', 'Wo')}
    del _L0_cond_all

    def _L1_cond_setup():
        import jax, jax.numpy as jnp
        import numpy as np
        HEADS = 16
        EPS = 1e-06

        def _rms_norm(x, g):
            xf = x.astype(jnp.float32)
            y = xf * jax.lax.rsqrt(jnp.mean(xf * xf, axis=-1, keepdims=True) + EPS)
            return y.astype(x.dtype) * g
        key = jax.random.key(seed)
        ks = jax.random.split(key, 6)
        b, n, dim, emb_dim = (4, 512, 512, 512)
        d_head = dim // HEADS
        return {'x': jax.random.normal(ks[0], (b, n, dim), jnp.float32), 'emb': jax.random.normal(ks[1], (b, 1, emb_dim), jnp.float32), 'W_emb': jax.random.normal(ks[2], (emb_dim, 2 * dim), jnp.float32) * emb_dim ** (-0.5), 'b_emb': jnp.zeros((2 * dim,), jnp.float32), 'g_norm': jnp.ones((dim,), jnp.float32), 'W_qkv': jax.random.normal(ks[3], (dim, 3 * dim), jnp.float32) * dim ** (-0.5), 'g_q': jnp.ones((d_head,), jnp.float32), 'g_k': jnp.ones((d_head,), jnp.float32), 'W_out': jax.random.normal(ks[4], (dim, dim), jnp.float32) * dim ** (-0.5)}
    _L1_cond_all = _L1_cond_setup()
    _L1_cond_in = {k: v for k, v in _L1_cond_all.items() if k in ('W_emb', 'b_emb', 'g_norm', 'W_qkv', 'g_q', 'g_k', 'W_out')}
    del _L1_cond_all

    def _L2_cond_setup():
        import jax, jax.numpy as jnp
        import numpy as np
        DT = 0.01
        EPSILON = 0.08
        ALPHA = 0.7
        BETA = 0.8
        CLAMP = 20.0
        B, T, N = (64, 128, 512)

        def _derivative(q, p, drive, coupling, bias):
            i_couple = jnp.tanh(q) @ coupling.T
            dq = q - q ** 3 / 3.0 - p + drive + i_couple + bias
            dp = EPSILON * (q + ALPHA - BETA * p)
            return (dq, dp)

        def _rk4_step(q, p, drive, coupling, bias):
            dq1, dp1 = _derivative(q, p, drive, coupling, bias)
            dq2, dp2 = _derivative(q + 0.5 * DT * dq1, p + 0.5 * DT * dp1, drive, coupling, bias)
            dq3, dp3 = _derivative(q + 0.5 * DT * dq2, p + 0.5 * DT * dp2, drive, coupling, bias)
            dq4, dp4 = _derivative(q + DT * dq3, p + DT * dp3, drive, coupling, bias)
            q_next = q + DT / 6.0 * (dq1 + 2 * dq2 + 2 * dq3 + dq4)
            p_next = p + DT / 6.0 * (dp1 + 2 * dp2 + 2 * dp3 + dp4)
            q_next = jnp.clip(q_next, -CLAMP, CLAMP)
            p_next = jnp.clip(p_next, -CLAMP, CLAMP)
            return (q_next, p_next)
        key = jax.random.key(seed)
        k1, k2, k3, k4 = jax.random.split(key, 4)
        return {'q0': jax.random.normal(k1, (B, N), dtype=jnp.float32), 'p0': jax.random.normal(k2, (B, N), dtype=jnp.float32), 'input_drive_seq': jax.random.normal(k3, (B, T, N), dtype=jnp.float32), 'coupling': jax.random.normal(k4, (N, N), dtype=jnp.float32) * 0.01, 'bias': jnp.zeros((N,), dtype=jnp.float32)}
    _L2_cond_all = _L2_cond_setup()
    _L2_cond_in = {k: v for k, v in _L2_cond_all.items() if k in ('coupling', 'bias')}
    del _L2_cond_all

    def _L3_cond_setup():
        import jax, jax.numpy as jnp
        import numpy as np
        B, T, D = (16, 128, 512)
        key = jax.random.key(seed)
        k0, k1, k2, k3 = jax.random.split(key, 4)
        scale = 1.0 / np.sqrt(D)
        return {'initial_state': jax.random.normal(k0, (B, D), jnp.float32), 'inputs': jax.random.normal(k1, (B, T, D), jnp.float32), 'W_ih': jax.random.normal(k2, (D, 3 * D), jnp.float32) * scale, 'W_hh': jax.random.normal(k3, (D, 3 * D), jnp.float32) * scale, 'b_ih': jnp.zeros((3 * D,), jnp.float32), 'b_hh': jnp.zeros((3 * D,), jnp.float32)}
    _L3_cond_all = _L3_cond_setup()
    _L3_cond_in = {k: v for k, v in _L3_cond_all.items() if k in ('W_ih', 'W_hh', 'b_ih', 'b_hh')}
    del _L3_cond_all
    return {'x': x, 'cond_2048': cond_2048, 'L0_cond_Wq': _L0_cond_in['Wq'], 'L0_cond_Wo': _L0_cond_in['Wo'], 'L1_cond_W_emb': _L1_cond_in['W_emb'], 'L1_cond_b_emb': _L1_cond_in['b_emb'], 'L1_cond_g_norm': _L1_cond_in['g_norm'], 'L1_cond_W_qkv': _L1_cond_in['W_qkv'], 'L1_cond_g_q': _L1_cond_in['g_q'], 'L1_cond_g_k': _L1_cond_in['g_k'], 'L1_cond_W_out': _L1_cond_in['W_out'], 'L2_cond_coupling': _L2_cond_in['coupling'], 'L2_cond_bias': _L2_cond_in['bias'], 'L3_cond_W_ih': _L3_cond_in['W_ih'], 'L3_cond_W_hh': _L3_cond_in['W_hh'], 'L3_cond_b_ih': _L3_cond_in['b_ih'], 'L3_cond_b_hh': _L3_cond_in['b_hh']}

def reference(x, cond_2048, L0_cond_Wq, L0_cond_Wo, L1_cond_W_emb, L1_cond_b_emb, L1_cond_g_norm, L1_cond_W_qkv, L1_cond_g_q, L1_cond_g_k, L1_cond_W_out, L2_cond_coupling, L2_cond_bias, L3_cond_W_ih, L3_cond_W_hh, L3_cond_b_ih, L3_cond_b_hh):
    import jax
    import jax.numpy as jnp

    def _L0_cond_ref(x, mask, Wq, Wo):
        import jax, jax.numpy as jnp
        import numpy as np
        NH = 8
        NEG = -1e+30
        B, D, T = x.shape
        dk = D // NH
        scale = 1.0 / jnp.sqrt(jnp.asarray(dk, x.dtype))
        xt = jnp.transpose(x, (0, 2, 1))
        q = xt @ Wq.T
        qh = q.reshape(B, T, NH, dk).transpose(0, 2, 1, 3)
        scores = scale * jnp.einsum('bhqd,bhkd->bhqk', qh, qh)
        cmask = mask[:, None, None, :]
        rmask = mask[:, None, :, None]
        logits = (scores * cmask + (1.0 - cmask) * NEG) * rmask
        attn = jax.nn.softmax(logits, axis=-1)
        ctx = jnp.einsum('bhqk,bhkd->bhqd', attn, qh)
        ctx = ctx.transpose(0, 2, 1, 3).reshape(B, T, D)
        out = ctx @ Wo.T
        return jnp.transpose(out, (0, 2, 1))

    def _L1_cond_ref(x, emb, W_emb, b_emb, g_norm, W_qkv, g_q, g_k, W_out):
        import jax, jax.numpy as jnp
        import numpy as np
        HEADS = 16
        EPS = 1e-06

        def _rms_norm(x, g):
            xf = x.astype(jnp.float32)
            y = xf * jax.lax.rsqrt(jnp.mean(xf * xf, axis=-1, keepdims=True) + EPS)
            return y.astype(x.dtype) * g
        b, n, dim = x.shape
        h = HEADS
        d = dim // h
        scale_shift = emb @ W_emb + b_emb
        scale, shift = jnp.split(scale_shift, 2, axis=-1)
        xn = _rms_norm(x, g_norm) * (1.0 + scale) + shift
        qkv = xn @ W_qkv
        qkv = qkv.reshape(b, n, 3, h, d)
        q, k, v = jnp.moveaxis(qkv, 2, 0)
        q = jnp.swapaxes(q, 1, 2)
        k = jnp.swapaxes(k, 1, 2)
        v = jnp.swapaxes(v, 1, 2)
        q = _rms_norm(q, g_q)
        k = _rms_norm(k, g_k)
        logits = jnp.einsum('bhqd,bhkd->bhqk', q, k) * d ** (-0.5)
        attn = jax.nn.softmax(logits, axis=-1)
        o = jnp.einsum('bhqk,bhkd->bhqd', attn, v)
        o = jnp.swapaxes(o, 1, 2).reshape(b, n, dim)
        return o + o @ W_out

    def _L2_cond_ref(q0, p0, input_drive_seq, coupling, bias):
        import jax, jax.numpy as jnp
        import numpy as np
        DT = 0.01
        EPSILON = 0.08
        ALPHA = 0.7
        BETA = 0.8
        CLAMP = 20.0
        B, T, N = (64, 128, 512)

        def _derivative(q, p, drive, coupling, bias):
            i_couple = jnp.tanh(q) @ coupling.T
            dq = q - q ** 3 / 3.0 - p + drive + i_couple + bias
            dp = EPSILON * (q + ALPHA - BETA * p)
            return (dq, dp)

        def _rk4_step(q, p, drive, coupling, bias):
            dq1, dp1 = _derivative(q, p, drive, coupling, bias)
            dq2, dp2 = _derivative(q + 0.5 * DT * dq1, p + 0.5 * DT * dp1, drive, coupling, bias)
            dq3, dp3 = _derivative(q + 0.5 * DT * dq2, p + 0.5 * DT * dp2, drive, coupling, bias)
            dq4, dp4 = _derivative(q + DT * dq3, p + DT * dp3, drive, coupling, bias)
            q_next = q + DT / 6.0 * (dq1 + 2 * dq2 + 2 * dq3 + dq4)
            p_next = p + DT / 6.0 * (dp1 + 2 * dp2 + 2 * dp3 + dp4)
            q_next = jnp.clip(q_next, -CLAMP, CLAMP)
            p_next = jnp.clip(p_next, -CLAMP, CLAMP)
            return (q_next, p_next)
        drive_tbn = jnp.swapaxes(input_drive_seq, 0, 1)

        def scan_fn(carry, drive):
            q, p = carry
            q, p = _rk4_step(q, p, drive, coupling, bias)
            return ((q, p), q)
        (_, _), q_trace_tbn = jax.lax.scan(scan_fn, (q0, p0), drive_tbn)
        return jnp.swapaxes(q_trace_tbn, 0, 1)

    def _L3_cond_ref(initial_state, inputs, W_ih, W_hh, b_ih, b_hh):
        import jax, jax.numpy as jnp
        import numpy as np
        B, T, D = (16, 128, 512)
        "ScanOverTime(GRU cell): sequential per-timestep module call with\n            dict-state passing; merge_dict_trees stacks the per-step\n            'state_predicted' tensors along axis=1 -> [B, T, D]."

        def cell(h, x):
            gi = x @ W_ih + b_ih
            gh = h @ W_hh + b_hh
            i_r, i_z, i_n = jnp.split(gi, 3, axis=-1)
            h_r, h_z, h_n = jnp.split(gh, 3, axis=-1)
            r = jax.nn.sigmoid(i_r + h_r)
            z = jax.nn.sigmoid(i_z + h_z)
            n = jnp.tanh(i_n + r * h_n)
            h_new = (1.0 - z) * n + z * h
            return (h_new, h_new)
        xs = jnp.swapaxes(inputs, 0, 1)
        _, hs = jax.lax.scan(cell, initial_state, xs)
        return jnp.swapaxes(hs, 0, 1)
    x = x + _L0_cond_ref(x, cond_2048, L0_cond_Wq, L0_cond_Wo)
    x = x + _L1_cond_ref(x, cond_2048[:, None, :], L1_cond_W_emb, L1_cond_b_emb, L1_cond_g_norm, L1_cond_W_qkv, L1_cond_g_q, L1_cond_g_k, L1_cond_W_out)
    x = x + _L2_cond_ref(cond_2048, cond_2048, x, L2_cond_coupling, L2_cond_bias)
    x = x + _L3_cond_ref(cond_2048, x, L3_cond_W_ih, L3_cond_W_hh, L3_cond_b_ih, L3_cond_b_hh)
    return x

_drawn_inputs = setup_inputs


def setup_inputs(seed=0):
    import zlib

    import numpy as np

    out = dict(_drawn_inputs(seed))
    spreads = {'L1_cond_b_emb': (0.0, 0.1),
     'L1_cond_g_norm': (1.0, 0.2),
     'L1_cond_g_q': (1.0, 0.6),
     'L1_cond_g_k': (1.0, 0.6),
     'L2_cond_bias': (0.0, 0.1),
     'L3_cond_b_ih': (0.0, 0.49),
     'L3_cond_b_hh': (0.0, 0.763)}
    factors = {}
    for name, (base, spread) in spreads.items():
        noise = np.random.default_rng([zlib.crc32(name.encode()), seed]).standard_normal(out[name].shape)
        drawn = base * np.exp(spread * noise) if base else spread * noise
        out[name] = jnp.asarray(drawn.astype(out[name].dtype))
    for name, factor in factors.items():
        out[name] = (out[name] * factor).astype(out[name].dtype)
    return out
```

```python
from contextlib import ExitStack

import concourse.bass as bass
from concourse import mybir
ALU = mybir.AluOpType
ACT = mybir.ActivationFunctionType
F32 = mybir.dt.float32
F16 = mybir.dt.float16

P = 128
B = 8
T = 256
D = 512
C = D // P
CB = C * B
STEPS = 8
CH = 4
BODIES = T // STEPS
CHUNKS = T // CH
SC = 64.0

DT, EPSILON, ALPHA, BETA, CLAMP = 0.01, 0.08, 0.7, 0.8, 20.0
SHIFT = ALPHA / BETA
A_Q = [DT / 2, DT / 2, DT, DT / 6]


def recurrences(nc, sb, sem, psum, X, Wc, Wh, Wi, vec, out):
    bank_L2, bank_R, bank_N, bank_Z, bank_G = psum[0], psum[1], psum[2], psum[3], psum[4:6]
    ps2 = bank_L2[:, 0:2 * CB].rearrange("p (w c b) -> p w c b", w=2, c=C)
    gate_ps = [x[:, 0:2 * CB].rearrange("p (w c b) -> p w c b", w=2, c=C) for x in (bank_R, bank_N, bank_Z)]
    NG = 3 * C
    GU = NG // CH
    gi_ps = [x[:, 0:GU * 2 * CH * B].rearrange("p (g w n) -> p g w n", g=GU, w=2) for x in bank_G]

    st = lambda name: sb(name, [P, C, B], F32)
    q = [st(f"q{s + 1}") for s in range(4)]
    q_next = st("q_next")
    p = [st(f"p{s + 1}") for s in range(4)]
    p_next = st("p_next")
    tanh32, cube, square, base, known, with_lo, pull = (st(x) for x in ("tanh32", "cube", "square", "base", "known", "with_lo", "pull"))
    q_third, p_third, q_sum, p_sum, q_avg, p_avg = (st(x) for x in ("q_third", "p_third", "q_sum", "p_sum", "q_avg", "p_avg"))
    drive_p = [st(f"drive_p{k}") for k in range(2)]
    rest = [st(f"rest{k}") for k in range(2)]
    thl = sb("tanh_parts", [P, C, 2, B], F16)
    hhl = sb("h_parts", [P, C, 2, B], F16)
    h, cand, tr, tz, r_pre, z_pre, r_lo, z_lo, n_lo, hn, rhn, n_pre, h_n, zh = (
        st(x) for x in ("h", "cand", "tanh_r", "tanh_z", "r_pre", "z_pre", "r_lo", "z_lo", "n_lo", "hn", "rhn", "n_pre", "h_minus_n", "zh"))
    bhn = st("b_hn")
    xr = [sb(f"x_chunk{k}", [P, C, CH, B], F32) for k in range(2)]
    dr = [sb(f"drive{k}", [P, C, CH, B], F32) for k in range(2)]
    x2 = [sb(f"x2_{k}", [P, C, CH, B], F32) for k in range(2)]
    x2p = [sb(f"x2_parts{k}", [P, C, 2, CH * B], F16) for k in range(2)]
    gi = [sb(f"gi{k}", [P, NG, CH, B], F32) for k in range(2)]
    yo = [sb(f"y{k}", [P, C, CH, B], F32) for k in range(2)]
    drive_bias = sb("drive_bias", [P, C, CH, B], F32)

    names = """q_ready q0_ready p_ready p0_ready tanh_hi tanh32_ready tanh_lo square_ready cube_ready base_ready
        known_ready with_lo_ready pull_ready q_third_ready p_third_ready  c2_done
        drive_p_ready rest_ready q_sum_ready p_sum_ready q_avg_ready p_avg_ready
        x_chunk_ready drive_ready x2_ready x2_hi_ready x2_parts_ready y_ready y_stored0 y_stored1
        r_done n_done z_done gi_done gi_biased gi_ready
        r_lo_ready r_pre_ready n_lo_ready hn_ready rhn_ready n_pre_ready z_lo_ready z_pre_ready zh_ready
        tr_ready cand_ready tz_ready h_n_ready h_ready h_hi_ready h_lo_ready p_raw_ready init_done""".split()
    S = {n: sem(n) for n in names}

    def wait(e, name, value):
        if isinstance(value, int) and value <= 0:
            return
        e.wait_ge(S[name], value)

    flat = lambda a: a[:].rearrange("p c b -> p (c b)")

    def l2_low(e):
        for c in range(C):
            for k in range(C):
                e.matmul(ps2[:, 0, c, :], Wc[1][:, k, c * P:(c + 1) * P], thl[:, k, 0, :],
                         start=(c == 0 and k == 0), stop=False, skip_group_check=True)

    def l2_high(e):
        for c in range(C):
            for k in range(C):
                mm = e.matmul(ps2[:, :, c, :], Wc[0][:, k, c * P:(c + 1) * P], thl[:, k, :, :],
                              start=False, stop=(c == C - 1 and k == C - 1), skip_group_check=True)
        return mm

    def l3_products(e, u, first, last):
        for x in range(first, last):
            gate, y = divmod(x, 2 * C * C)
            part, y = divmod(y, C * C)
            c, k = divmod(y, C)
            col = (0, 2, 1)[gate] * D + c * P
            if x == 0:
                wait(e, "h_hi_ready", u + 1)
            if x == C * C:
                wait(e, "h_lo_ready", u + 1)
            if part == 0:
                mm = e.matmul(gate_ps[gate][:, 0, c, :], Wh[1][:, k, col:col + P], hhl[:, k, 0, :],
                              start=(y == 0), stop=False, skip_group_check=True)
            else:
                mm = e.matmul(gate_ps[gate][:, :, c, :], Wh[0][:, k, col:col + P], hhl[:, k, :, :],
                              start=False, stop=(y == C * C - 1), skip_group_check=True)
            if part == 1 and y == C * C - 1:
                mm.then_inc(S[("r_done", "n_done", "z_done")[gate]], 1)

    def gi_products(e, v, kappa, par, first, last):
        for x in range(first, last):
            g, y = divmod(x, 2 * C)
            k, part = divmod(y, 2)
            gg, bank = g, kappa % 2
            g += kappa * GU
            if x == 0:
                wait(e, "gi_ready", v - 1)
            if x == 0 and kappa == 0:
                wait(e, "x2_parts_ready", v + CH)
            if part == 0:
                mm = e.matmul(gi_ps[bank][:, gg, :, :], Wi[0][:, k, g * P:(g + 1) * P], x2p[par][:, k, :, :],
                              start=(gg == 0 and k == 0), stop=False, skip_group_check=True)
            else:
                mm = e.matmul(gi_ps[bank][:, gg, 0, :], Wi[1][:, k, g * P:(g + 1) * P], x2p[par][:, k, 0, :],
                              start=False, stop=(k == C - 1), skip_group_check=True)
        if last == 2 * C * GU:
            mm.then_inc(S["gi_done"], 1)

    def tensor_step(e, i, tau, l2, l3, gi_now, gi_before):
        t, u, v = i * STEPS + tau, (i - 1) * STEPS + tau, i * STEPS + tau - CH
        kappa, par = tau % CH, (tau // CH + 1) % 2
        for s in range(4):
            n = t * 4 + s
            if l2:
                wait(e, "tanh_hi", n + 1)
                l2_low(e)
            if s == 0 and gi_before:
                gi_products(e, v - 1, (tau - 1) % CH, ((tau - 1) // CH + 1) % 2, 19, 24)
            if l3 and s:
                l3_products(e, u, *((25, 30), (55, 60), (85, 90))[s - 1])
            if l2:
                wait(e, "tanh_lo", n + 1)
                l2_high(e).then_inc(S["c2_done"], 1)
            if l3:
                l3_products(e, u, *((0, 25), (30, 55), (60, 85), (90, 96))[s])
        if gi_now:
            gi_products(e, v, kappa, par, 0, 19)

    def tanh_of(e, n, src, src_sq, sq_sem, sq_value):
        wait(e, "q_ready", n + 1)
        e.activation(thl[:, :, 0, :], src[:], ACT.Tanh).then_inc(S["tanh_hi"], 1)
        e.activation(tanh32[:], src[:], ACT.Tanh).then_inc(S["tanh32_ready"], 1)
        wait(e, sq_sem, sq_value)
        e.activation(square[:], src_sq[:], ACT.Square).then_inc(S["square_ready"], 1)

    def scalar_step(e, i, tau, l2, l3, gi_before):
        t, u, v = i * STEPS + tau, (i - 1) * STEPS + tau, i * STEPS + tau - CH
        half = tau // CH
        for s in range(4):
            n = t * 4 + s
            if s == 0 and gi_before:
                wait(e, "gi_done", v)
                k0 = (tau - 1) % CH
                for gg in range(GU):
                    g = k0 * GU + gg
                    ins = e.activation(gi[((tau - 1) // CH + 1) % 2][:, g, :, :].rearrange("p t b -> p (t b)"),
                                       gi_ps[k0 % 2][:, gg, 0, :], ACT.Identity, bias=vec["b_gates"][:, g:g + 1], scale=1 / SC)
                ins.then_inc(S["gi_biased"], 1)
            if s == 1 and l2 and tau % CH == 2:
                wait(e, "x2_ready", t - 2)
                e.activation(xr[(half + 1) % 2][:].rearrange("p c t b -> p c (t b)"),
                             X[:, :, bass.ds((i * 2 + (half + 1)) * CH * B, CH * B)], ACT.Copy).then_inc(S["x_chunk_ready"], 1)
            if s == 3 and l2:
                wait(e, "q_sum_ready", t + 1)
                e.activation(q_avg[:], q_sum[:], ACT.Copy, scale=1 / 3).then_inc(S["q_avg_ready"], 1)
                wait(e, "p_sum_ready", t + 1)
                e.activation(p_avg[:], p_sum[:], ACT.Copy, scale=1 / 3).then_inc(S["p_avg_ready"], 1)
            if s == 3 and l3:
                wait(e, "n_pre_ready", u + 1)
                e.activation(cand[:], n_pre[:], ACT.Tanh).then_inc(S["cand_ready"], 1)
            if l2:
                if s < 3:
                    tanh_of(e, n + 1, q[s + 1], q[s + 1], "q_ready", n + 2)
                else:
                    tanh_of(e, n + 1, q_next, q[0], "q0_ready", t + 2)
            if s == 1 and l3:
                wait(e, "r_pre_ready", u + 1)
                e.activation(tr[:], r_pre[:], ACT.Tanh, scale=0.5).then_inc(S["tr_ready"], 1)
        if l3:
            wait(e, "z_pre_ready", u + 1)
            e.activation(tz[:], z_pre[:], ACT.Tanh, scale=0.5).then_inc(S["tz_ready"], 1)
            wait(e, "h_ready", u + 2)
            e.activation(hhl[:, :, 0, :], h[:], ACT.Copy).then_inc(S["h_hi_ready"], 1)

    def vector_step(e, i, tau, l2, l3, gi_before):
        t, u, v = i * STEPS + tau, (i - 1) * STEPS + tau, i * STEPS + tau - CH
        kappa, gpar = tau % CH, (tau // CH) % 2
        stt = e.scalar_tensor_tensor
        for s in range(4):
            n = t * 4 + s
            a = A_Q[s]
            if l2:
                wait(e, "p_ready" if s else "p0_ready", t * 3 + s if s else t + 1)
                wait(e, "q_ready" if s else "q0_ready", n + 1 if s else t + 1)
                stt(out=flat(pull), in0=flat(p[s]), scalar=-BETA, in1=flat(q[s]), op0=ALU.mult, op1=ALU.add).then_inc(S["pull_ready"], 1)
                wait(e, "square_ready", n + 1)
                stt(out=flat(cube), in0=flat(square), scalar=-1 / 3, in1=flat(q[s]), op0=ALU.mult, op1=ALU.mult).then_inc(S["cube_ready"], 1)
                if s == 3:
                    wait(e, "q_avg_ready", t + 1)
                    stt(out=flat(q_third), in0=flat(q[3]), scalar=1 / 3, in1=flat(q_avg), op0=ALU.mult, op1=ALU.add).then_inc(S["q_third_ready"], 1)
                    wait(e, "p_avg_ready", t + 1)
                    stt(out=flat(p_third), in0=flat(p[3]), scalar=1 / 3, in1=flat(p_avg), op0=ALU.mult, op1=ALU.add).then_inc(S["p_third_ready"], 1)
                    wait(e, "q_third_ready", t + 1)
                wait(e, "rest_ready", n + 1)
                stt(out=flat(base), in0=flat(rest[s % 2]), scalar=a, in1=flat(q_third if s == 3 else q[0]),
                    op0=ALU.mult, op1=ALU.add).then_inc(S["base_ready"], 1)
                wait(e, "pull_ready", n + 1)
                if s < 3:
                    stt(out=flat(p[s + 1]), in0=flat(pull), scalar=A_Q[s] * EPSILON, in1=flat(p[0]),
                        op0=ALU.mult, op1=ALU.add).then_inc(S["p_ready"], 1)
                else:
                    wait(e, "p_third_ready", t + 1)
                    stt(out=flat(p_next), in0=flat(pull), scalar=DT / 6 * EPSILON, in1=flat(p_third),
                        op0=ALU.mult, op1=ALU.add).then_inc(S["p_raw_ready"], 1)
                wait(e, "base_ready", n + 1)
                wait(e, "cube_ready", n + 1)
                stt(out=flat(known), in0=flat(cube), scalar=a, in1=flat(base), op0=ALU.mult, op1=ALU.add).then_inc(S["known_ready"], 1)
                if s == 3:
                    wait(e, "p_raw_ready", t + 1)
                    e.tensor_scalar(flat(p[0]), flat(p_next), CLAMP - SHIFT, -CLAMP - SHIFT, ALU.min, ALU.max).then_inc(S["p0_ready"], 1)
            if s == 0 and l3:
                wait(e, "h_hi_ready", u + 1)
                e.tensor_tensor(hhl[:, :, 1, :], h[:], hhl[:, :, 0, :], ALU.subtract).then_inc(S["h_lo_ready"], 1)
            if s == 0 and gi_before:
                wait(e, "gi_biased", v)
                k0 = (tau - 1) % CH
                dst = gi[((tau - 1) // CH + 1) % 2][:, k0 * GU:(k0 + 1) * GU, :, :].rearrange("p g t b -> p g (t b)")
                stt(out=dst, in0=gi_ps[k0 % 2][:, :, 1, :], scalar=1 / SC, in1=dst,
                    op0=ALU.mult, op1=ALU.add).then_inc(S["gi_ready"], 1)
            if s == 3 and l3:
                wait(e, "tr_ready", u + 1)
                wait(e, "hn_ready", u + 1)
                stt(out=flat(rhn), in0=flat(tr), scalar=1.0, in1=flat(hn), op0=ALU.add, op1=ALU.mult).then_inc(S["rhn_ready"], 1)
                wait(e, "rhn_ready", u + 1)
                stt(out=n_pre[:], in0=rhn[:], scalar=0.5, in1=gi[gpar][:, 2 * C:3 * C, kappa, :], op0=ALU.mult, op1=ALU.add).then_inc(S["n_pre_ready"], 1)
            if l2:
                wait(e, "c2_done", n + 1)
                wait(e, "known_ready", n + 1)
                stt(out=with_lo[:], in0=ps2[:, 1, :, :], scalar=a / SC, in1=known[:], op0=ALU.mult, op1=ALU.add).then_inc(S["with_lo_ready"], 1)
                wait(e, "with_lo_ready", n + 1)
                nxt = q[s + 1] if s < 3 else q_next
                stt(out=nxt[:], in0=ps2[:, 0, :, :], scalar=a / SC, in1=with_lo[:], op0=ALU.mult, op1=ALU.add).then_inc(S["q_ready"], 1)
                if s == 3:
                    wait(e, "q_ready", n + 2)
                    e.tensor_scalar(flat(q[0]), flat(q_next), CLAMP, -CLAMP, ALU.min, ALU.max).then_inc(S["q0_ready"], 1)
            if l3 and s:
                gate = s - 1
                lo, full, src = ((r_lo, r_pre, "r"), (n_lo, hn, "n"), (z_lo, z_pre, "z"))[gate]
                other = bhn[:] if gate == 1 else gi[gpar][:, (0 if gate == 0 else C):(C if gate == 0 else 2 * C), kappa, :]
                if gate == 0 and kappa == 0:
                    wait(e, "gi_ready", u + CH)
                wait(e, src + "_done", u + 1)
                stt(out=lo[:], in0=gate_ps[gate][:, 1, :, :], scalar=1 / SC, in1=other, op0=ALU.mult, op1=ALU.add).then_inc(S[src + "_lo_ready"], 1)
                wait(e, src + "_lo_ready", u + 1)
                stt(out=full[:], in0=gate_ps[gate][:, 0, :, :], scalar=1 / SC, in1=lo[:], op0=ALU.mult, op1=ALU.add)\
                    .then_inc(S["hn_ready" if gate == 1 else src + "_pre_ready"], 1)
            if l2:
                wait(e, "tanh32_ready", n + 2)
                e.tensor_tensor(thl[:, :, 1, :], tanh32[:], thl[:, :, 0, :], ALU.subtract).then_inc(S["tanh_lo"], 1)
        if l3:
            wait(e, "tz_ready", u + 1)
            wait(e, "h_n_ready", u + 1)
            stt(out=flat(zh), in0=flat(tz), scalar=1.0, in1=flat(h_n), op0=ALU.add, op1=ALU.mult).then_inc(S["zh_ready"], 1)
            wait(e, "zh_ready", u + 1)
            stt(out=flat(h), in0=flat(zh), scalar=0.5, in1=flat(cand), op0=ALU.mult, op1=ALU.add).then_inc(S["h_ready"], 1)

    def gpsimd_step(e, i, tau, l2, l3):
        t, u = i * STEPS + tau, (i - 1) * STEPS + tau
        half, kappa = tau // CH, tau % CH
        tt = e.tensor_tensor
        for s in range(4):
            n = t * 4 + s
            if l2 and s == 1:
                tt(flat(q_third_sum), flat(q[1]), flat(q[0]), ALU.subtract).then_inc(S["q_sum1"], 1)
                tt(flat(p_third_sum), flat(p[1]), flat(p[0]), ALU.subtract).then_inc(S["p_sum1"], 1)
                if kappa == 2:
                    wait(e, "x_chunk_ready", i * 2 + (half + 2))
                    o = (half + 1) % 2
                    tt(dr[o][:].rearrange("p c t b -> p (c t b)"), xr[o][:].rearrange("p c t b -> p (c t b)"),
                       drive_bias[:].rearrange("p c t b -> p (c t b)"), ALU.add).then_inc(S["drive_ready"], 1)
            if l2 and s == 2:
                wait(e, "q_sum1", t + 1)
                tt(flat(q_sum2), flat(q_third_sum), flat(q[2]), ALU.add).then_inc(S["q_sum2s"], 1)
                wait(e, "p_sum1", t + 1)
                tt(flat(p_sum2), flat(p_third_sum), flat(p[2]), ALU.add).then_inc(S["p_sum2s"], 1)
                wait(e, "q_sum2s", t + 1)
                tt(flat(q_sum), flat(q_sum2), flat(q[2]), ALU.add).then_inc(S["q_sum_ready"], 1)
                wait(e, "p_sum2s", t + 1)
                tt(flat(p_sum), flat(p_sum2), flat(p[2]), ALU.add).then_inc(S["p_sum_ready"], 1)
            if l3 and s == 3:
                wait(e, "cand_ready", u + 1)
                tt(flat(h_n), flat(h), flat(cand), ALU.subtract).then_inc(S["h_n_ready"], 1)
            if l2:
                if s < 3:
                    wait(e, "p_ready", t * 3 + s + 1)
                    d = dr[half][:, :, kappa, :]
                else:
                    wait(e, "p0_ready", t + 2)
                    d = dr[((tau + 1) // CH) % 2][:, :, (tau + 1) % CH, :]
                    if kappa == CH - 1:
                        wait(e, "drive_ready", i * 2 + (half + 2))
                tt(drive_p[(s + 1) % 2][:], d, p[(s + 1) % 4][:], ALU.subtract).then_inc(S["drive_p_ready"], 1)
                if s < 3:
                    wait(e, "q_ready", n + 2)
                else:
                    wait(e, "q0_ready", t + 2)
                wait(e, "drive_p_ready", n + 2)
                tt(flat(rest[(s + 1) % 2]), flat(drive_p[(s + 1) % 2]), flat(q[(s + 1) % 4]), ALU.add).then_inc(S["rest_ready"], 1)
        if l3:
            wait(e, "h_ready", u + 2)
            if kappa == 0:
                wait(e, f"y_stored{half}", i * 16)
            tt(yo[half][:, :, kappa, :], x2[half][:, :, kappa, :], h[:], ALU.add).then_inc(S["y_ready"], 1)
        if l2:
            if l3:
                wait(e, "y_ready", u + 1)
            tt(x2[half][:, :, kappa, :], xr[half][:, :, kappa, :], q[0][:], ALU.add).then_inc(S["x2_ready"], 1)
            hi = x2p[half][:, :, 0, kappa * B:(kappa + 1) * B]
            tt(hi, xr[half][:, :, kappa, :], q[0][:], ALU.add).then_inc(S["x2_hi_ready"], 1)
            wait(e, "x2_hi_ready", t + 1)
            tt(x2p[half][:, :, 1, kappa * B:(kappa + 1) * B], x2[half][:, :, kappa, :], hi, ALU.subtract).then_inc(S["x2_parts_ready"], 1)

    q_third_sum, p_third_sum, q_sum2, p_sum2 = (st(x) for x in ("q_sum1_", "p_sum1_", "q_sum2_", "p_sum2_"))
    for x in ("q_sum1", "p_sum1", "q_sum2s", "p_sum2s"):
        S[x] = sem(x)

    def vector_start(e):
        cond = vec["cond_t"]
        e.tensor_copy(flat(q[0]), cond).then_inc(S["q0_ready"], 1)
        e.tensor_copy(flat(q_next), cond).then_inc(S["q_ready"], 1)
        e.tensor_copy(flat(h), cond).then_inc(S["h_ready"], 1)
        e.tensor_scalar(flat(p[0]), cond, -SHIFT, None, ALU.add).then_inc(S["p0_ready"], 1)
        for c in range(C):
            e.memset(bhn[:, c, :], 0.0)
        for c in range(C):
            e.memset(drive_bias[:, c, :, :], -SHIFT)
        for k in range(2):
            e.memset(yo[k][:], 0.0).then_inc(S[f"y_stored{k}"], 16)
        e.memset(X[:, :, T * B:(T + CH) * B], 0.0).then_inc(S["init_done"], 1)
        wait(e, "init_done", 1)
        for c in range(C):
            e.tensor_scalar(bhn[:, c, :], bhn[:, c, :], vec["b_hn"][:, c:c + 1], None, ALU.add)
        for c in range(C):
            w = drive_bias[:, c, :, :].rearrange("p t b -> p (t b)")
            ins = e.tensor_scalar(w, w, vec["bias2"][:, c:c + 1], None, ALU.add)
        ins.then_inc(S["init_done"], 1)
        wait(e, "init_done", 2)

    def vector_first_lo(e):
        wait(e, "tanh32_ready", 1)
        e.tensor_tensor(thl[:, :, 1, :], tanh32[:], thl[:, :, 0, :], ALU.subtract).then_inc(S["tanh_lo"], 1)

    def scalar_start(e):
        e.activation(xr[0][:].rearrange("p c t b -> p c (t b)"), X[:, :, 0:CH * B], ACT.Copy).then_inc(S["x_chunk_ready"], 1)
        tanh_of(e, 0, q_next, q[0], "q0_ready", 1)
        wait(e, "h_ready", 1)
        e.activation(hhl[:, :, 0, :], h[:], ACT.Copy).then_inc(S["h_hi_ready"], 1)

    def gpsimd_start(e):
        wait(e, "x_chunk_ready", 1)
        wait(e, "init_done", 2)
        tt = e.tensor_tensor
        tt(dr[0][:].rearrange("p c t b -> p (c t b)"), xr[0][:].rearrange("p c t b -> p (c t b)"),
           drive_bias[:].rearrange("p c t b -> p (c t b)"), ALU.add).then_inc(S["drive_ready"], 1)
        wait(e, "drive_ready", 1)
        wait(e, "p0_ready", 1)
        tt(drive_p[0][:], dr[0][:, :, 0, :], p[0][:], ALU.subtract).then_inc(S["drive_p_ready"], 1)
        wait(e, "q0_ready", 1)
        wait(e, "drive_p_ready", 1)
        tt(flat(rest[0]), flat(drive_p[0]), flat(q[0]), ALU.add).then_inc(S["rest_ready"], 1)

    def wait_ready(e, keys):
        for k in keys:
            e.wait_ge(*ready[k])

    def run(e, step, l3_gi):
        step(e, 0, "first")
        with e.Fori(1, BODIES) as i:
            step(e, i, "loop")
        step(e, BODIES, "last")

    def has(which, tau):
        l2 = which != "last"
        l3 = which != "first"
        gi_now = which == "loop" or (which == "first" and tau >= CH) or (which == "last" and tau < CH)
        gi_before = which == "loop" or (which == "first" and tau > CH) or (which == "last" and tau <= CH)
        return l2, l3, gi_now, gi_before

    def tensor(e):
        def body(e, i, which):
            for tau in range(STEPS):
                tensor_step(e, i, tau, *has(which, tau))
        run(e, body, None)

    def scalar(e):
        scalar_start(e)
        def body(e, i, which):
            for tau in range(STEPS):
                l2, l3, _, before = has(which, tau)
                scalar_step(e, i, tau, l2, l3, before)
        run(e, body, None)

    def vector(e):
        vector_first_lo(e)
        def body(e, i, which):
            for tau in range(STEPS):
                l2, l3, _, before = has(which, tau)
                vector_step(e, i, tau, l2, l3, before)
        run(e, body, None)

    def gpsimd(e):
        gpsimd_start(e)
        def body(e, i, which):
            for tau in range(STEPS):
                l2, l3, _, _ = has(which, tau)
                gpsimd_step(e, i, tau, l2, l3)
        run(e, body, None)

    def sync(e):
        def store(e, jj, par):
            at = jj if isinstance(jj, int) else e.snap(jj)
            wait(e, "y_ready", jj * CH + CH)
            e.dma_start(out[:, bass.ds(at, 1), :],
                        yo[par][:].rearrange("p c t b -> p (c t b)").rearrange("p (o n) -> p o n", o=1)).then_inc(S[f"y_stored{par}"], 16)
        with e.Fori(1, BODIES) as i:
            store(e, (i - 1) * 2, 0)
            store(e, (i - 1) * 2 + 1, 1)
        store(e, (BODIES - 1) * 2, 0)
        store(e, (BODIES - 1) * 2 + 1, 1)
        for k in range(2):
            wait(e, f"y_stored{k}", 16 * (BODIES + 1))

    return dict(tensor=tensor, scalar=scalar, vector=vector, gpsimd=gpsimd, sync=sync, vector_start=vector_start, S=S)


SEQ_A, HEADS_A, DIM_A = 512, 8, 256
SEQ_B, HEADS_B, DIM_B = 256, 16, 512
DH = 32
NEG = -1e30
ROWS = 3 * DH
MAX_SCALE = 64.0
WALL = C * (D + 3 * D)
ARENA = 34816
UNIT = WALL // 8


def per_batch(b, per, plus):
    i, k = b
    return i * (2 * per) + (k * per + plus)


def wait_pos(e, sem, value):
    if isinstance(value, int) and value <= 0:
        return
    e.wait_ge(sem, value)


def attention_core(name, sem, psum, heads, keys, QK, V, prob, mx, mrow, ident, ctx, rec, mask_bias):
    per = 512 // keys
    tiles = heads * (keys // 128) // per
    bank_s, bank_t, bank_o = psum[2:4], psum[4:6], psum[6:8]
    half = tiles // 2
    names = """score0_done score1_done score0_free score1_free max_ready maxT_row shift_ready packed
        weights_scores exp_done pv_done head_done head_free rec_ready ctx_ready""".split()
    S = {n: sem(f"{name}_{n}") for n in names}
    LAG = 2
    EXP0, PV0, FREE0 = 2, 4, 2

    first = tiles // 4 if keys == 512 else tiles // 2
    after = {x: [] for x in range(tiles)}
    for j in range(tiles):
        after[first + (tiles - first) * j // tiles].append(j)

    def block(x):
        return (x * per // (keys // 128), x * per % (keys // 128))

    class Core:
        sems = S

        @staticmethod
        def prime(e):
            e.nop().then_inc(S["exp_done"], EXP0)
            e.nop().then_inc(S["pv_done"], PV0)
            e.nop().then_inc(S["head_free"], FREE0)

        @staticmethod
        def score_tile(e, b, par, j):
            s = j % 2
            wait_pos(e, S[f"score{s}_free"], per_batch(b, half + (s == 0), j // 2))
            if j == 0:
                e.wait_ge(S["packed"], per_batch(b, 16 * 24, 16 * 24))
            h, blk = block(j)
            for y in range(per):
                mm = e.matmul(bank_s[s][:, y * keys:(y + 1) * keys], QK[par][0][0:ROWS, h, (blk + y) * 128:(blk + y + 1) * 128],
                              QK[par][1][0:ROWS, h, :], start=True, stop=True)
            mm.then_inc(S[f"score{s}_done"], 1)

        @staticmethod
        def max_tile(e, b, j):
            s = j % 2
            e.wait_ge(S[f"score{s}_done"], per_batch(b, half + (s == 0), j // 2 + 1))
            e.tensor_reduce(mx[:, j * per:(j + 1) * per], bank_s[s][:, :].rearrange("p (y k) -> p y k", y=per),
                            mybir.AxisListType.X, ALU.max).then_inc(S[f"score{s}_free"], 1)

        @staticmethod
        def max_rows(e, b):
            wait_pos(e, S["score0_free"], per_batch(b, half + 1, half))
            e.wait_ge(S["score1_free"], per_batch(b, half, half))
            e.transpose(bank_s[0][0:32, 0:128], mx[:, :], ident[:, :]).then_inc(S["score0_done"], 1)

        @staticmethod
        def shift_rows(e, b):
            e.wait_ge(S["score0_done"], per_batch(b, half + 1, half + 1))
            wait_pos(e, S["maxT_row"], per_batch(b, 16, 0))
            e.activation(mrow[:, :], bank_s[0][0:32, 0:128], ACT.Copy, scale=-1 / MAX_SCALE).then_inc(S["score0_free"], 1)

        @staticmethod
        def move_shift(e, b, par):
            e.wait_ge(S["score0_free"], per_batch(b, half + 1, half + 1))
            e.dma_start(QK[par][0][ROWS:ROWS + 1, :, :].rearrange("p h q -> p (h q)"), mrow[:, :]).then_inc(S["maxT_row"], 16)

        @staticmethod
        def weight_tile(e, b, par, x):
            if x == 0:
                e.wait_ge(S["maxT_row"], per_batch(b, 16, 16))
            e.wait_ge(S["exp_done"], per_batch(b, tiles, x - 1 + EXP0))
            h, blk = block(x)
            for y in range(per):
                mm = e.matmul(bank_t[x % 2][:, y * keys:(y + 1) * keys], QK[par][1][0:ROWS + 1, h, (blk + y) * 128:(blk + y + 1) * 128],
                              QK[par][0][0:ROWS + 1, h, :], start=True, stop=True)
            mm.then_inc(S["weights_scores"], 1)

        @staticmethod
        def exp_tile(e, b, x, par):
            e.wait_ge(S["weights_scores"], per_batch(b, tiles, x + 1))
            e.wait_ge(S["pv_done"], per_batch(b, tiles, x - 3 + PV0))
            bias = {} if mask_bias is None else dict(bias=mask_bias[par][:, x % 4:x % 4 + 1])
            e.activation(prob[x % 4][:, :], bank_t[x % 2][:, :], ACT.Exp, scale=DH ** -0.5, **bias).then_inc(S["exp_done"], 1)

        @staticmethod
        def pv_tile(e, b, par, x, extra=None):
            h, blk = block(x)
            kb = keys // 128
            if blk == 0:
                e.wait_ge(S["head_free"], per_batch(b, heads, h - 1 + FREE0))
            e.wait_ge(S["exp_done"], per_batch(b, tiles, x + 1 + EXP0))
            out = bank_o[h % 2][0:2 * DH, 0:keys]
            for y in range(per):
                mm = e.matmul(out, V[par][:, blk + y, h, :], prob[x % 4][:, y * keys:(y + 1) * keys],
                              start=(blk + y == 0), stop=(blk + y == kb - 1 and extra is None))
            mm.then_inc(S["pv_done"], 1)
            if blk + per == kb:
                if extra is not None:
                    mm = e.matmul(out, extra[0], extra[1], start=False, stop=True)
                mm.then_inc(S["head_done"], 1) if extra is not None else None

        @staticmethod
        def divide(e, b, h):
            if heads == HEADS_A:
                e.wait_ge(S["head_done"], per_batch(b, heads, h + 1))
            else:
                e.wait_ge(S["pv_done"], per_batch(b, tiles, h + 1 + PV0))
            po = bank_o[h % 2]
            j, g = h % 4, h // 4
            e.reciprocal(rec[h % 2][0:DH, 0:keys], po[DH:2 * DH, 0:keys]).then_inc(S["rec_ready"], 1)
            e.wait_ge(S["rec_ready"], per_batch(b, heads, h + 1))
            e.tensor_tensor(ctx[DH * j:DH * (j + 1), g, :], po[0:DH, 0:keys], rec[h % 2][0:DH, 0:keys], ALU.mult)\
             .then_inc(S["head_free"], 1)

    Core.EXP0, Core.PV0, Core.FREE0 = EXP0, PV0, FREE0
    Core.tiles, Core.after, Core.first, Core.LAG = tiles, after, first, LAG
    return Core


def pack(e, core, b, QKp, parts, heads):
    qh, ql, kh, kl = parts
    for side, blocks in ((0, (qh, qh, ql)), (1, (kh, kl, kh))):
        for row, src in enumerate(blocks):
            for j in range(4):
                dst = QKp[side][row * DH:(row + 1) * DH, :, :].rearrange("p (g j) q -> p g j q", j=4)[:, :, j, :]
                e.dma_start(dst, src[j * DH:(j + 1) * DH, :, :]).then_inc(core.sems["packed"], 16)


def build(nc, a):
    with ExitStack() as stack:
        def sb(name, shape, dt):
            return stack.enter_context(nc.sbuf_tensor("sb_" + name, shape, dt))

        def sem(name):
            return stack.enter_context(nc.semaphore(name))

        psum = [stack.enter_context(nc.psum_tensor(f"bank{k}", [P, 512], F32)) for k in range(8)]

        X = sb("X", [P, C, (T + CH) * B], F32)
        w_parts = [sb(f"w_parts{k}", [P, WALL], F16) for k in range(2)]
        arena = sb("arena", [P, ARENA], F32)
        ident = sb("ident", [P, P], F32)
        cond_t = sb("cond_t", [P, C * B], F32)
        ssq = sb("ssq", [P, 2 * B], F32)
        rstd = sb("rstd", [P, 2 * B], F32)
        head_ones = sb("head_ones", [P, P], F32)
        guard_w = sb("guard_w", [1, 2 * DH], F16)
        mx = sb("mx", [P, 32], F32)
        mrow = sb("mrow", [32, P], F16)
        mask_col = [sb(f"mask_col{k}", [P, 4], F32) for k in range(2)]
        mask_bias = [sb(f"mask_bias{k}", [P, 4], F32) for k in range(2)]
        v_sum = [sb(f"v_sum{k}", [P, 2], F32) for k in range(2)]
        g_q, g_k = sb("g_q", [P, 1], F32), sb("g_k", [P, 1], F32)
        g_norm = sb("g_norm", [P, C], F32)
        b_emb = sb("b_emb", [P, 2 * C], F32)
        eps = sb("eps", [P, 1], F32)
        mod = sb("mod", [P, 2 * C, B], F32)
        mod_b = [sb(f"mod_b{k}", [P, 2 * C], F32) for k in range(2)]
        bias2 = sb("bias2", [P, C], F32)
        b_ih, b_hh, b_gates = (sb(x, [P, 3 * C], F32) for x in ("b_ih", "b_hh", "b_gates"))

        def cut(at, shape, dt=F32):
            n = 1
            for x in shape:
                n *= x
            cols = n * (2 if dt is F16 else 4) // 4
            v = arena[:, at:at + cols]
            if dt is F16:
                v = v.bitcast(F16)
            names = "abc"[:len(shape)]
            if len(shape) > 1:
                v = v.rearrange(f"p ({' '.join(names)}) -> p {' '.join(names)}", **{m: s for m, s in zip(names, shape)})
            return v, at + cols

        x_flat = X[:, :, :].rearrange("p c n -> p (c n)")
        w_emb = x_flat[:, 0:4 * 1024].rearrange("p (k n) -> p k n", k=C)
        stage = [x_flat[:, 4096 + k * UNIT:4096 + (k + 1) * UNIT] for k in range(2)]

        at = 0
        xb, xres, qk_a, v_a, prob_a, crow, irow, irow16, rec_a = [], [], [], [], [], [], [], [], []
        for k in range(2):
            v, at = cut(at, (2, SEQ_A)); xb.append(v)
        xres, at = cut(at, (2, SEQ_A))
        wq, at = cut(at, (2, DIM_A))
        wo, at = cut(at, (2, DIM_A))
        parts_a = []
        for k in range(4):
            v, at = cut(at, (2, SEQ_A), F16); parts_a.append(v)
        for k in range(2):
            u, at = cut(at, (HEADS_A, SEQ_A), F16)
            v, at = cut(at, (HEADS_A, SEQ_A), F16)
            qk_a.append((u, v))
        for k in range(2):
            v, at = cut(at, (4, HEADS_A, 2 * DH)); v_a.append(v)
        for k in range(4):
            v, at = cut(at, (512,)); prob_a.append(v)
        for k in range(2):
            v, at = cut(at, (SEQ_A,)); crow.append(v)
            v, at = cut(at, (SEQ_A,)); irow.append(v)
            v, at = cut(at, (SEQ_A,), F16); irow16.append(v)
            v, at = cut(at, (SEQ_A,)); rec_a.append(v)
        squares = []
        for k in range(2):
            v, at = cut(at, (SEQ_A,), F16); squares.append(v)
        ctx_a, at = cut(at, (2, SEQ_A))
        assert at <= ARENA - 1540
        CA = attention_core("a", sem, psum, HEADS_A, SEQ_A, qk_a, v_a, prob_a, mx, mrow, ident, ctx_a, rec_a, mask_bias)

        A = {n: sem("a_" + n) for n in """weights_in ident_ready start_ready res_in pj0_done pj1_done pj0_free pj1_free
            q_hi_ready q_lo_ready k_masked row_ready row_scaled bias_ready split_hi split_done v_ready
            blend0 blended added res_used""".split()}
        for n in ("x_in", "mask_in", "stage_in"):
            A[n] = [sem(f"a_{n}{k}") for k in range(2)]

        at = 0
        wqkv, at = cut(at, (C, 3 * D))
        after_wqkv = at
        raw, at = cut(at, (8, SEQ_B))
        sq, at = cut(at, (4, 512))
        xnT, at = cut(at, (C, SEQ_B))
        xs, at = cut(at, (2, D))
        parts_b = []
        for k in range(4):
            v, at = cut(at, (4, SEQ_B), F16); parts_b.append(v)
        wout, at = cut(at, (C, D))
        x1 = []
        for k in range(2):
            v, at = cut(at, (2, D)); x1.append(v)
        qk_b, v_b, prob_b, rec_b = [], [], [], []
        after_x1 = at
        for k in range(2):
            u, at = cut(at, (HEADS_B, SEQ_B), F16)
            v, at = cut(at, (HEADS_B, SEQ_B), F16)
            qk_b.append((u, v))
        for k in range(2):
            v, at = cut(at, (2, HEADS_B, 2 * DH)); v_b.append(v)
        for k in range(4):
            v, at = cut(at, (512,)); prob_b.append(v)
        for k in range(2):
            v, at = cut(at, (SEQ_B,)); rec_b.append(v)
        ctx_b, at = cut(at, (C, SEQ_B))
        assert at <= ARENA
        CB_ = attention_core("b", sem, psum, HEADS_B, SEQ_B, qk_b, v_b, prob_b, mx, mrow, ident, ctx_b, rec_b, None)
        Bs = {n: sem("b_" + n) for n in """weights_in start_ready emb_in emb_done mod0 mod_ready rstd0 rstd_ready xs_ready modb_ready
            pj0_done pj1_done pj0_free pj1_free sq_ready raw_ready root_ready inv_ready norm_ready hi_ready lo_ready xn_ready v_ready
            x_written wih_in wih_hi wih_done""".split()}
        Bs["x1_in"] = [sem(f"b_x1_in{k}") for k in range(2)]

        c_at = [after_x1]

        def sbc(name, shape, dt):
            v, c_at[0] = cut(c_at[0], tuple(shape[1:]), dt)
            return v
        wih_parts = []
        at = after_wqkv
        for k in range(2):
            v, at = cut(at, (C, 3 * D), F16); wih_parts.append(v)
        assert at <= after_wqkv + 7168
        cw = [w_parts[k][:, 0:C * D].rearrange("p (k n) -> p k n", k=C) for k in range(2)]
        hw = [w_parts[k][:, C * D:WALL].rearrange("p (k n) -> p k n", k=C) for k in range(2)]
        R = recurrences(nc, sbc, sem, psum, X, cw, hw, wih_parts,
                        dict(cond_t=cond_t[:, :], b_gates=b_gates, b_hn=b_hh[:, 2 * C:3 * C], bias2=bias2), a["out"])
        assert c_at[0] <= ARENA

        block = stack.enter_context(nc.Block())

        def pairs(e, body, last):
            with e.Fori(0, B // 2 - 1) as i:
                for k in range(2):
                    body(e, (i, k), True)
            body(e, (B // 2 - 1, 0), True)
            last(e, (B // 2 - 1, 1), False)

        def nxt(b):
            return (b[0], 1) if b[1] == 0 else (b[0] + 1, 0)

        def index(b):
            return per_batch(b, 1, 0)

        def proj_job(b, first, per, at, nxt_there=True):
            return per_batch(b, per, first + at)

        @block.sync
        def _(e):
            x_d = a["x"].rearrange("b (k p) t -> b p k t", p=P)

            def at_batch(n):
                return n if isinstance(n, int) else e.snap(n)

            def wait_all(*waits):
                values = [(s, v if isinstance(v, int) else e.snap(v)) for s, v in waits]
                for s, v in values:
                    wait_pos(e, s, v)

            def load_x(n, par):
                e.dma_start(xb[par], x_d[bass.ds(n, 1)].rearrange("o p k t -> (o p) k t")).then_inc(A["x_in"][par], 16)

            def load_mask(n, par):
                e.dma_start(crow[par], a["cond"][bass.ds(n, 1), :].rearrange("o t -> (o t)").partition_broadcast(P)).then_inc(A["mask_in"][par], 16)
                e.dma_start(mask_col[par][:, :], a["cond_cols"][bass.ds(n, 1)].rearrange("o p k -> (o p) k")).then_inc(A["mask_in"][par], 16)

            load_x(0, 0)
            e.dma_start(wq, a["wq_t"].rearrange("(k p) n -> p k n", p=P)).then_inc(A["weights_in"], 16)
            load_mask(0, 0)
            load_x(1, 1)
            load_mask(1, 1)
            e.dma_start(wo, a["wo_t"].rearrange("(k p) n -> p k n", p=P)).then_inc(A["weights_in"], 16)
            e.dma_start(cond_t[:, :], a["cond_t"]).then_inc(Bs["emb_in"], 16)
            e.dma_start(w_emb, a["w_emb"].rearrange("(k p) n -> p k n", p=P)).then_inc(Bs["emb_in"], 16)
            for dst, src in ((b_emb, "b_emb"), (g_norm, "g_norm"), (bias2, "bias2"), (b_ih, "b_ih"), (b_hh, "b_hh")):
                e.dma_start(dst[:, :], a[src]).then_inc(Bs["emb_in"], 16)
            for dst, src in ((g_q, "g_q"), (g_k, "g_k")):
                for j in range(4):
                    e.dma_start(dst[j * DH:(j + 1) * DH, :], a[src].rearrange("(p o) -> p o", o=1)).then_inc(Bs["emb_in"], 16)

            def pack_a(b, par):
                wait_all((A["k_masked"], per_batch(b, 2, 2)), (CA.sems["pv_done"], per_batch(b, CA.tiles, CA.PV0 - CA.tiles)))
                pack(e, CA, b, qk_a[par], parts_a, HEADS_A)

            def one(e, b, more):
                par, other = b[1], 1 - b[1]
                n, n2, unit = at_batch(index(b)), at_batch(index(b) + 2), at_batch(index(b) * UNIT)
                e.wait_ge(A["split_done"], per_batch(b, 1, 1))
                e.dma_start(stage[par], a["wall"][:, bass.ds(unit, UNIT)]).then_inc(A["stage_in"][par], 16)
                more2 = more and not (isinstance(b[0], int) and b[1] == 0)
                if more2:
                    e.wait_ge(A["v_ready"], per_batch(b, 4, 4))
                    load_x(n2, par)
                if more:
                    pack_a(nxt(b), other)
                e.wait_ge(A["res_used"], per_batch(b, 18, 18))
                e.dma_start(xres, x_d[bass.ds(n, 1)].rearrange("o p k t -> (o p) k t")).then_inc(A["res_in"], 16)
                if more:
                    CA.move_shift(e, nxt(b), other)
                if more2:
                    e.wait_ge(A["blended"], per_batch(b, 2, 2))
                    load_mask(n2, par)
                e.wait_ge(A["added"], per_batch(b, 2, 2))
                e.dma_start(a["x1"][bass.ds(n, 1)].rearrange("o p n -> (o p) n"), xres.rearrange("p k t -> p (k t)")).then_inc(A["res_used"], 16)

            pack_a((0, 0), 0)
            CA.move_shift(e, (0, 0), 0)
            with e.Fori(0, B // 2 - 1) as i:
                one(e, (i, 0), True)
                one(e, (i, 1), True)
            one(e, (B // 2 - 1, 0), True)
            one(e, (B // 2 - 1, 1), False)
            e.wait_ge(A["res_used"], 18 * B + 18)

            e.wait_ge(A["res_used"], 18 * B + 18)
            e.dma_start(wqkv, a["w_qkv"].rearrange("(k p) n -> p k n", p=P)).then_inc(Bs["weights_in"], 16)

            def load_x1(n, par):
                e.dma_start(x1[par], a["x1"][bass.ds(n, 1)].rearrange("o p (k t) -> (o p) k t", k=2)).then_inc(Bs["x1_in"][par], 16)

            load_x1(0, 0)
            load_x1(1, 1)
            e.dma_start(wout, a["w_out"].rearrange("(k p) n -> p k n", p=P)).then_inc(Bs["weights_in"], 16)

            def pack_b(b, par):
                wait_all((Bs["lo_ready"], per_batch(b, 4, 4)), (CB_.sems["pv_done"], per_batch(b, CB_.tiles, CB_.PV0 - CB_.tiles)))
                pack(e, CB_, b, qk_b[par], parts_b, HEADS_B)

            def one_b(e, b, more):
                par, other = b[1], 1 - b[1]
                n2 = at_batch(index(b) + 2)
                if more:
                    pack_b(nxt(b), other)
                    CB_.move_shift(e, nxt(b), other)
                if more and not (isinstance(b[0], int) and b[1] == 0):
                    e.wait_ge(Bs["x_written"], per_batch(b, 4, 4))
                    load_x1(n2, par)

            pack_b((0, 0), 0)
            CB_.move_shift(e, (0, 0), 0)
            with e.Fori(0, B // 2 - 1) as i:
                one_b(e, (i, 0), True)
                one_b(e, (i, 1), True)
            one_b(e, (B // 2 - 1, 0), True)
            e.wait_ge(Bs["v_ready"], 2 * B)
            e.wait_ge(Bs["raw_ready"], 4 * B)
            e.dma_start(wqkv, a["w_ih"].rearrange("(k p) n -> p k n", p=P)).then_inc(Bs["wih_in"], 16)
            R["sync"](e)

        @block.tensor
        def _(e):
            pj = psum[0:2]

            def pj_wait(S, bank, job):
                wait_pos(e, S[f"pj{bank}_free"], job)

            def project_a(b, par, j0):
                e.wait_ge(A["x_in"][b[1]], b[0] * 16 + 16)
                for g in range(2):
                    pj_wait(A, g, j0)
                    for k in range(2):
                        mm = e.matmul(pj[g][:, :], wq[:, k, g * P:(g + 1) * P], xb[par][:, k, :], start=k == 0, stop=k == 1)
                    mm.then_inc(A[f"pj{g}_done"], 1)
                for g in range(2):
                    pj_wait(A, g, j0 + 1)
                    for y in range(2):
                        t = 2 * g + y
                        for k in range(2):
                            mm = e.matmul(pj[g][:, y * DIM_A:(y + 1) * DIM_A], xb[par][:, k, t * P:(t + 1) * P], wq[:, k, :],
                                          start=k == 0, stop=k == 1)
                    mm.then_inc(A[f"pj{g}_done"], 1)

            def out_a(b, par, j):
                e.wait_ge(A["blended"], per_batch(b, 2, 2))
                for n in range(2):
                    pj_wait(A, n, j)
                    for g in range(2):
                        mm = e.matmul(pj[n][:, :], wo[:, g, n * P:(n + 1) * P], ctx_a[:, g, :], start=g == 0, stop=g == 1)
                    mm.then_inc(A[f"pj{n}_done"], 1)

            def attend(core, b, par, more, extra):
                for x in range(core.tiles + core.LAG):
                    if x < core.tiles:
                        core.weight_tile(e, b, par, x)
                    if x >= core.LAG:
                        core.pv_tile(e, b, par, x - core.LAG, extra(par) if extra else None)
                    if more and x < core.tiles:
                        for j in core.after[x]:
                            core.score_tile(e, nxt(b), 1 - par, j)

            def first_scores(core):
                for j in range(core.tiles):
                    core.score_tile(e, (0, 0), 0, j)
                core.max_rows(e, (0, 0))

            e.wait_ge(A["weights_in"], 32)
            e.wait_ge(A["start_ready"], 12)
            e.wait_ge(A["ident_ready"], 5)
            project_a((0, 0), 0, 0)
            e.wait_ge(Bs["emb_in"], 16 * 15)
            emb = psum[6]
            for n in range(2 * C):
                for k in range(C):
                    mm = e.matmul(emb[:, n * B:(n + 1) * B], w_emb[:, k, n * P:(n + 1) * P], cond_t[:, k * B:(k + 1) * B], start=k == 0, stop=k == C - 1)
            mm.then_inc(Bs["emb_done"], 1)
            first_scores(CA)
            e.wait_ge(Bs["mod_ready"], 2)

            def batch_a(e, b, more):
                par = b[1]
                if more:
                    project_a(nxt(b), 1 - par, per_batch(b, 3, 2))
                attend(CA, b, par, more, lambda k: (guard_w[:, :], irow16[k][0:1, :]))
                if more:
                    CA.max_rows(e, nxt(b))
                out_a(b, par, per_batch(b, 3, 4 if more else 2))

            pairs(e, batch_a, batch_a)

            e.wait_ge(Bs["start_ready"], 1)

            def project_b(b, par, j0):
                e.wait_ge(Bs["xs_ready"], per_batch(b, 2, 2))
                for g in range(2):
                    pj_wait(Bs, g, j0)
                    for y in range(2):
                        f = 2 * g + y
                        for t in range(2):
                            mm = e.transpose(pj[g][:, y * SEQ_B + t * P:y * SEQ_B + (t + 1) * P], xs[:, t, f * P:(f + 1) * P], ident[:, :])
                    mm.then_inc(Bs[f"pj{g}_done"], 1)
                e.wait_ge(Bs["xn_ready"], per_batch(b, 4, 4))
                e.wait_ge(Bs["weights_in"], 32)
                for y in range(4):
                    pj_wait(Bs, y % 2, j0 + 1 + y // 2)
                    for z in range(2):
                        o = 2 * y + z
                        for k in range(C):
                            mm = e.matmul(pj[y % 2][:, z * SEQ_B:(z + 1) * SEQ_B], wqkv[:, k, o * P:(o + 1) * P], xnT[:, k, :],
                                          start=k == 0, stop=k == C - 1)
                    mm.then_inc(Bs[f"pj{y % 2}_done"], 1)
                    if y >= 2:
                        mean_squares(b, y - 2, j0)
                for t in range(2):
                    pj_wait(Bs, t, j0 + 4)
                    for k in range(C):
                        mm = e.matmul(pj[t][:, :], xnT[:, k, t * P:(t + 1) * P], wqkv[:, k, 2 * D:3 * D], start=k == 0, stop=k == C - 1)
                    mm.then_inc(Bs[f"pj{t}_done"], 1)
                for y in range(2, 4):
                    mean_squares(b, y, j0)

            def mean_squares(b, y, j0):
                pj_wait(Bs, y % 2, j0 + (3 if y < 2 else 5))
                e.wait_ge(Bs["sq_ready"], per_batch(b, 4, y + 1))
                e.matmul(pj[y % 2][:, :], head_ones[:, :], sq[:, y, :], start=True, stop=True).then_inc(Bs[f"pj{y % 2}_done"], 1)

            def out_b(b, par, j):
                e.wait_ge(CB_.sems["head_free"], per_batch(b, HEADS_B, HEADS_B + CB_.FREE0))
                for g in range(2):
                    pj_wait(Bs, g, j)
                    for z in range(2):
                        c = 2 * g + z
                        for k in range(C):
                            e.matmul(pj[g][:, z * SEQ_B:(z + 1) * SEQ_B], wout[:, k, c * P:(c + 1) * P], ctx_b[:, k, :],
                                     start=k == 0, stop=False)
                        for t in range(2):
                            mm = e.matmul(pj[g][:, z * SEQ_B + t * P:z * SEQ_B + (t + 1) * P], x1[par][:, t, c * P:(c + 1) * P], ident[:, :],
                                          start=False, stop=t == 1)
                    mm.then_inc(Bs[f"pj{g}_done"], 1)

            project_b((0, 0), 0, 0)
            first_scores(CB_)

            def batch_b(e, b, more):
                par = b[1]
                if more:
                    project_b(nxt(b), 1 - par, per_batch(b, 7, 6))
                attend(CB_, b, par, more, None)
                if more:
                    CB_.max_rows(e, nxt(b))
                out_b(b, par, per_batch(b, 7, 12 if more else 6))

            pairs(e, batch_b, batch_b)
            e.wait_ge(R["S"]["init_done"], 2)
            e.wait_ge(Bs["wih_done"], 1)
            R["tensor"](e)

        @block.scalar
        def _(e):
            pj = psum[0:2]

            def project_a(b, par, j0):
                for g in range(2):
                    e.wait_ge(A[f"pj{g}_done"], j0 + 1)
                    wait_pos(e, CA.sems["packed"], per_batch(b, 16 * 24, 0))
                    e.activation(parts_a[0][:, g, :], pj[g][:, :], ACT.Identity, accum_out=v_sum[par][:, g:g + 1]).then_inc(A["q_hi_ready"], 1)
                for g in range(2):
                    e.wait_ge(A[f"pj{g}_done"], j0 + 2)
                    for y in range(2):
                        ins = e.activation(v_a[par][:, 2 * g + y, :, 0:DH], pj[g][:, y * DIM_A:(y + 1) * DIM_A].rearrange("p (h d) -> p h d", d=DH), ACT.Copy)
                        ins.then_inc(A["v_ready"], 1)
                    ins = None
                    e.wait_ge(A["v_ready"], per_batch(b, 4, 2 * g + 2))
                    e.nop().then_inc(A[f"pj{g}_free"], 1)

            def batch_a(e, b, more):
                par = b[1]
                if more:
                    project_a(nxt(b), 1 - par, per_batch(b, 3, 2))
                e.wait_ge(A["bias_ready"], per_batch(b, 1, 1))
                for x in range(CA.tiles):
                    CA.exp_tile(e, b, x, par)
                if more:
                    CA.shift_rows(e, nxt(b))
                for k in range(2):
                    e.wait_ge(A["added"], per_batch(b, 2, k + 1))
                    e.activation(squares[k], xres[:, k, :], ACT.Square, accum_out=ssq[:, bass.ds(index(b) * 2 + k, 1)]).then_inc(A["res_used"], 1)

            project_a((0, 0), 0, 0)
            CA.shift_rows(e, (0, 0))
            pairs(e, batch_a, batch_a)

            e.wait_ge(A["res_used"], 18 * B + 18)
            e.activation(rstd[:, :], ssq[:, :], ACT.Sqrt, scale=1 / D, bias=eps[:, :]).then_inc(Bs["rstd0"], 1)
            e.wait_ge(Bs["start_ready"], 1)

            def project_b(b, par, j0):
                e.wait_ge(Bs["modb_ready"], per_batch(b, 1, 1))
                for g in range(2):
                    e.wait_ge(Bs[f"pj{g}_done"], j0 + 1)
                    for y in range(2):
                        f = 2 * g + y
                        ins = e.activation(xnT[:, f, :], pj[g][:, y * SEQ_B:(y + 1) * SEQ_B], ACT.Identity,
                                           scale=mod_b[par][:, f:f + 1], bias=mod_b[par][:, C + f:C + f + 1])
                        ins.then_inc(Bs["xn_ready"], 1)
                    e.wait_ge(Bs["xn_ready"], per_batch(b, 4, 2 * g + 2))
                    e.nop().then_inc(Bs[f"pj{g}_free"], 1)
                for y in range(4):
                    e.wait_ge(Bs[f"pj{y % 2}_done"], j0 + 2 + y // 2)
                    wait_pos(e, Bs["lo_ready"], per_batch(b, 4, 0))
                    e.activation(raw[:, 2 * y:2 * y + 2, :].rearrange("p a n -> p (a n)"), pj[y % 2][:, :], ACT.Copy).then_inc(Bs["raw_ready"], 1)
                    e.activation(sq[:, y, :], pj[y % 2][:, :], ACT.Square).then_inc(Bs["sq_ready"], 1)
                    e.wait_ge(Bs["raw_ready"], per_batch(b, 4, y + 1))
                    e.wait_ge(Bs["sq_ready"], per_batch(b, 4, y + 1))
                    e.nop().then_inc(Bs[f"pj{y % 2}_free"], 1)
                for y in range(2):
                    root(b, y, j0)
                for t in range(2):
                    e.wait_ge(Bs[f"pj{t}_done"], j0 + 5)
                    e.activation(v_b[par][:, t, :, 0:DH], pj[t][:, :].rearrange("p (h d) -> p h d", d=DH), ACT.Copy).then_inc(Bs["v_ready"], 1)
                    e.wait_ge(Bs["v_ready"], per_batch(b, 2, t + 1))
                    e.nop().then_inc(Bs[f"pj{t}_free"], 1)
                for y in range(2, 4):
                    root(b, y, j0)

            def root(b, y, j0):
                e.wait_ge(Bs[f"pj{y % 2}_done"], j0 + (4 if y < 2 else 6))
                e.activation(sq[:, y, :], pj[y % 2][:, :], ACT.Sqrt, bias=eps[:, :]).then_inc(Bs["root_ready"], 1)
                e.wait_ge(Bs["root_ready"], per_batch(b, 4, y + 1))
                e.nop().then_inc(Bs[f"pj{y % 2}_free"], 1)

            def batch_b(e, b, more):
                par = b[1]
                if more:
                    project_b(nxt(b), 1 - par, per_batch(b, 7, 6))
                for x in range(CB_.tiles):
                    CB_.exp_tile(e, b, x, par)
                if more:
                    CB_.shift_rows(e, nxt(b))

            project_b((0, 0), 0, 0)
            CB_.shift_rows(e, (0, 0))
            pairs(e, batch_b, batch_b)

            e.wait_ge(Bs["wih_in"], 16)
            e.activation(wih_parts[0].rearrange("p k n -> p (k n)"), wqkv.rearrange("p k n -> p (k n)"), ACT.Copy, scale=SC).then_inc(Bs["wih_hi"], 1)
            e.wait_ge(Bs["x_written"], 4 * B)
            e.wait_ge(R["S"]["init_done"], 2)
            R["scalar"](e)

        @block.vector
        def _(e):
            pj = psum[0:2]
            e.memset(head_ones[:, :], 0.0).then_inc(A["start_ready"], 1)
            e.wait_ge(A["start_ready"], 1)
            for j in range(4):
                e.memset(head_ones[j * DH:(j + 1) * DH, j * DH:(j + 1) * DH], 1.0 / DH).then_inc(A["start_ready"], 1)
            for k in range(2):
                e.memset(v_a[k][:, :, :, DH:2 * DH], 1.0).then_inc(A["start_ready"], 1)
                e.memset(qk_a[k][1][ROWS:ROWS + 1, :, :], MAX_SCALE).then_inc(A["start_ready"], 1)
            e.memset(eps[:, :], 1e-6).then_inc(A["start_ready"], 1)
            e.memset(guard_w[:, 0:DH], 0.0).then_inc(A["start_ready"], 1)
            e.memset(guard_w[:, DH:2 * DH], 1.0).then_inc(A["start_ready"], 1)

            def low_a(b, par, j0):
                for g in range(2):
                    e.wait_ge(A["q_hi_ready"], per_batch(b, 2, g + 1))
                    e.tensor_tensor(parts_a[1][:, g, :], pj[g][:, :], parts_a[0][:, g, :], ALU.subtract).then_inc(A["q_lo_ready"], 1)
                    e.wait_ge(A["q_lo_ready"], per_batch(b, 2, g + 1))
                    e.nop().then_inc(A[f"pj{g}_free"], 1)

            def attend(core, b, more, blend):
                for x in range(core.tiles + core.LAG):
                    if x >= core.LAG:
                        y = x - core.LAG
                        per_head = core.tiles // (HEADS_A if core is CA else HEADS_B)
                        if y % per_head == per_head - 1:
                            core.divide(e, b, y // per_head)
                            if blend is not None and (y // per_head) % 4 == 3:
                                blend(b, y // per_head // 4)
                    if more and x < core.tiles:
                        for j in core.after[x]:
                            core.max_tile(e, nxt(b), j)

            def blend_a(b, g):
                e.wait_ge(CA.sems["head_free"], per_batch(b, HEADS_A, 4 * g + 4 + CA.FREE0))
                e.tensor_tensor(ctx_a[:, g, :], ctx_a[:, g, :], crow[b[1]][:, :], ALU.mult).then_inc(A["blend0"], 1)
                e.wait_ge(A["blend0"], per_batch(b, 2, g + 1))
                e.wait_ge(A["row_scaled"], per_batch(b, 1, 1))
                e.scalar_tensor_tensor(out=ctx_a[:, g, :], in0=irow[b[1]][:, :], scalar=v_sum[b[1]][:, g:g + 1], in1=ctx_a[:, g, :],
                                       op0=ALU.mult, op1=ALU.add).then_inc(A["blended"], 1)

            def batch_a(e, b, more):
                par = b[1]
                if more:
                    low_a(nxt(b), 1 - par, None)
                at = index(b) * UNIT
                e.wait_ge(A["stage_in"][b[1]], b[0] * 16 + 16)
                e.tensor_scalar(w_parts[0][:, bass.ds(at, UNIT)], stage[par], SC, None, ALU.mult).then_inc(A["split_hi"], 1)
                e.wait_ge(A["split_hi"], per_batch(b, 1, 1))
                e.scalar_tensor_tensor(out=w_parts[1][:, bass.ds(at, UNIT)], in0=stage[par], scalar=SC, in1=w_parts[0][:, bass.ds(at, UNIT)],
                                       op0=ALU.mult, op1=ALU.subtract).then_inc(A["split_done"], 1)
                attend(CA, b, more, blend_a)
                e.wait_ge(A["res_in"], per_batch(b, 16, 16))
                for k in range(2):
                    e.wait_ge(A[f"pj{k}_done"], per_batch(b, 3, 5 if more else 3))
                    e.tensor_tensor(xres[:, k, :], pj[k][:, :], xres[:, k, :], ALU.add).then_inc(A["added"], 1)
                    e.wait_ge(A["added"], per_batch(b, 2, k + 1))
                    e.nop().then_inc(A[f"pj{k}_free"], 1)

            low_a((0, 0), 0, 0)
            e.wait_ge(Bs["emb_done"], 1)
            emb = psum[6][:, 0:2 * C * B].rearrange("p (c b) -> p c b", b=B)
            e.tensor_tensor(mod[:, :, :], emb, b_emb[:, :].rearrange("p (c o) -> p c o", o=1).to_broadcast([P, 2 * C, B]), ALU.add).then_inc(Bs["mod_ready"], 1)
            e.wait_ge(Bs["mod_ready"], 1)
            e.tensor_scalar(mod[:, 0:C, :], mod[:, 0:C, :], 1.0, None, ALU.add).then_inc(Bs["mod0"], 1)
            e.wait_ge(Bs["mod0"], 1)
            e.tensor_tensor(mod[:, 0:C, :], mod[:, 0:C, :], g_norm[:, :].rearrange("p (c o) -> p c o", o=1).to_broadcast([P, C, B]), ALU.mult).then_inc(Bs["mod_ready"], 1)
            e.tensor_copy(b_gates[:, :], b_ih[:, :]).then_inc(Bs["mod0"], 1)
            e.wait_ge(Bs["mod0"], 2)
            e.tensor_tensor(b_gates[:, 0:2 * C], b_ih[:, 0:2 * C], b_hh[:, 0:2 * C], ALU.add)
            for j in range(CA.tiles):
                CA.max_tile(e, (0, 0), j)
            pairs(e, batch_a, batch_a)

            e.wait_ge(A["res_used"], 18 * B + 18)
            e.wait_ge(Bs["rstd0"], 1)
            e.reciprocal(rstd[:, :], rstd[:, :]).then_inc(Bs["rstd_ready"], 1)
            for k in range(2):
                e.memset(v_b[k][:, :, :, DH:2 * DH], 1.0).then_inc(Bs["rstd_ready"], 1)
                e.memset(qk_b[k][1][ROWS:ROWS + 1, :, :], MAX_SCALE).then_inc(Bs["rstd_ready"], 1)
            e.wait_ge(Bs["rstd_ready"], 5)
            e.nop().then_inc(Bs["start_ready"], 1)

            def scaled(b, par):
                e.wait_ge(Bs["x1_in"][b[1]], b[0] * 16 + 16)
                e.tensor_copy(mod_b[par][:, :].rearrange("p (c o) -> p c o", o=1), mod[:, :, bass.ds(index(b), 1)]).then_inc(Bs["modb_ready"], 1)
                wait_pos(e, Bs["xn_ready"], per_batch(b, 4, 0))
                for t in range(2):
                    e.tensor_scalar(xs[:, t, :], x1[par][:, t, :], rstd[:, bass.ds(index(b) * 2 + t, 1)], None, ALU.mult).then_inc(Bs["xs_ready"], 1)

            def normalise(b, y):
                e.wait_ge(Bs["root_ready"], per_batch(b, 4, y + 1))
                e.reciprocal(sq[:, y, :], sq[:, y, :]).then_inc(Bs["inv_ready"], 1)
                e.wait_ge(Bs["inv_ready"], per_batch(b, 4, y + 1))
                g = (g_q, g_k)[y // 2]
                flat2 = lambda v: v.rearrange("p a n -> p (a n)")
                src = flat2(raw[:, 2 * y:2 * y + 2, :])
                z = 2 * (y % 2)
                wait_pos(e, CB_.sems["packed"], per_batch(b, 16 * 24, 0))
                e.scalar_tensor_tensor(out=flat2(parts_b[2 * (y // 2)][:, z:z + 2, :]), in0=src, scalar=g[:, 0:1], in1=sq[:, y, :],
                                       op0=ALU.mult, op1=ALU.mult).then_inc(Bs["hi_ready"], 1)
                e.scalar_tensor_tensor(out=src, in0=src, scalar=g[:, 0:1], in1=sq[:, y, :],
                                       op0=ALU.mult, op1=ALU.mult).then_inc(Bs["norm_ready"], 1)

            def batch_b(e, b, more):
                par = b[1]
                if more:
                    for y in range(4):
                        normalise(nxt(b), y)
                attend(CB_, b, more, None)
                if more and not (isinstance(b[0], int) and b[1] == 0):
                    scaled((b[0] + 1, b[1]), par) if False else None
                for c in range(C):
                    e.wait_ge(Bs[f"pj{c // 2}_done"], per_batch(b, 7, 13 if more else 7))
                    z = c % 2
                    e.tensor_tensor(X[:, c, 0:T * B].rearrange("p (t b) -> p t b", b=B)[:, :, bass.ds(index(b), 1)],
                                    pj[c // 2][:, z * SEQ_B:(z + 1) * SEQ_B].rearrange("p (t o) -> p t o", o=1),
                                    ctx_b[:, c, :].rearrange("p (t o) -> p t o", o=1), ALU.add).then_inc(Bs["x_written"], 1)
                    if z == 1:
                        e.wait_ge(Bs["x_written"], per_batch(b, 4, c + 1))
                        e.nop().then_inc(Bs[f"pj{c // 2}_free"], 1)
                if more and not (isinstance(b[0], int) and b[1] == 0):
                    scaled((b[0] + 1, b[1]), par)

            scaled((0, 0), 0)
            for y in range(4):
                normalise((0, 0), y)
            scaled((0, 1), 1)
            for j in range(CB_.tiles):
                CB_.max_tile(e, (0, 0), j)
            pairs(e, batch_b, batch_b)

            e.wait_ge(Bs["wih_hi"], 1)
            e.scalar_tensor_tensor(out=wih_parts[1].rearrange("p k n -> p (k n)"), in0=wqkv.rearrange("p k n -> p (k n)"), scalar=SC,
                                   in1=wih_parts[0].rearrange("p k n -> p (k n)"), op0=ALU.mult, op1=ALU.subtract).then_inc(Bs["wih_done"], 1)
            R["vector_start"](e)
            R["vector"](e)

        @block.gpsimd
        def _(e):
            CA.prime(e)
            CB_.prime(e)
            e.nop().then_inc(A["split_done"], 2)
            e.nop().then_inc(A["res_used"], 18)
            e.memset(ident[:, :], 0.0).then_inc(A["ident_ready"], 1)
            e.wait_ge(A["ident_ready"], 1)
            e.affine_select(out=ident[:, :], in_=ident[:, :], compare_op=ALU.not_equal, fill=1.0, base=0,
                            pattern=[[-1, P]], channel_multiplier=1).then_inc(A["ident_ready"], 1)

            def masks(b, par):
                e.wait_ge(A["mask_in"][b[1]], b[0] * 32 + 32)
                e.tensor_tensor(tmp_row[:, :], one_row[:, :], crow[par][:, :], ALU.subtract).then_inc(A["row_ready"], 1)
                e.wait_ge(A["row_ready"], per_batch(b, 1, 1))
                e.tensor_tensor(irow[par][:, :], tmp_row[:, :], over_row[:, :], ALU.mult)
                e.tensor_tensor(irow16[par][0:1, :], one_row[0:1, :], crow[par][0:1, :], ALU.subtract).then_inc(A["row_scaled"], 1)
                e.tensor_tensor(mask_bias[par][:, :], mask_col[par][:, :], big[:, :], ALU.mult).then_inc(A["bias0"], 1)
                e.wait_ge(A["bias0"], per_batch(b, 1, 1))
                e.tensor_tensor(mask_bias[par][:, :], mask_bias[par][:, :], big[:, :], ALU.subtract).then_inc(A["bias_ready"], 1)
                for g in range(2):
                    e.wait_ge(A["q_hi_ready"], per_batch(b, 2, g + 1))
                    e.tensor_tensor(parts_a[2][:, g, :], parts_a[0][:, g, :], crow[par][:, :], ALU.mult)
                    e.wait_ge(A["q_lo_ready"], per_batch(b, 2, g + 1))
                    e.tensor_tensor(parts_a[3][:, g, :], parts_a[1][:, g, :], crow[par][:, :], ALU.mult).then_inc(A["k_masked"], 1)

            A["bias0"] = sem("a_bias0")
            one_row, _x = cut(ARENA - 1540, (SEQ_A,))
            over_row, _x = cut(ARENA - 1028, (SEQ_A,))
            tmp_row, _x = cut(ARENA - 516, (SEQ_A,))
            big, _x = cut(ARENA - 4, (4,))
            e.memset(one_row[:, :], 1.0).then_inc(A["ident_ready"], 1)
            e.memset(over_row[:, :], 1.0 / SEQ_A).then_inc(A["ident_ready"], 1)
            e.memset(big[:, :], -NEG).then_inc(A["ident_ready"], 1)
            e.wait_ge(A["ident_ready"], 5)
            masks((0, 0), 0)

            def batch_a(e, b, more):
                if more:
                    masks(nxt(b), 1 - b[1])

            pairs(e, batch_a, batch_a)

            def low_b(b):
                for y in range(4):
                    e.wait_ge(Bs["norm_ready"], per_batch(b, 4, y + 1))
                    z = 2 * (y % 2)
                    e.tensor_tensor(parts_b[2 * (y // 2) + 1][:, z:z + 2, :], raw[:, 2 * y:2 * y + 2, :], parts_b[2 * (y // 2)][:, z:z + 2, :],
                                    ALU.subtract).then_inc(Bs["lo_ready"], 1)

            low_b((0, 0))

            def batch_b(e, b, more):
                if more:
                    low_b(nxt(b))

            pairs(e, batch_b, batch_b)
            e.wait_ge(Bs["x_written"], 4 * B)
            e.wait_ge(R["S"]["init_done"], 2)
            R["gpsimd"](e)


def kernel(x, cond_2048, L0_cond_Wq, L0_cond_Wo, L1_cond_W_emb, L1_cond_b_emb, L1_cond_g_norm, L1_cond_W_qkv, L1_cond_g_q, L1_cond_g_k,
           L1_cond_W_out, L2_cond_coupling, L2_cond_bias, L3_cond_W_ih, L3_cond_W_hh, L3_cond_b_ih, L3_cond_b_hh):
    import numpy as np
    import concourse.bacc as bacc
    from concourse.bass_utils import run_bass_kernel_spmd as launch

    flat = np.ascontiguousarray
    rows = lambda w: np.asarray(w).reshape(C, P, -1).transpose(1, 0, 2).reshape(P, -1)
    cols = lambda v: flat(np.asarray(v).reshape(-1, P).T)
    cond = np.asarray(cond_2048)
    arrays = dict(
        x=x, cond=cond,
        cond_t=flat(rows(cond.T)),
        cond_cols=flat(cond.reshape(B, C, P).transpose(0, 2, 1)),
        wq_t=flat(np.asarray(L0_cond_Wq).T), wo_t=flat(np.asarray(L0_cond_Wo).T),
        w_emb=L1_cond_W_emb, b_emb=cols(L1_cond_b_emb), g_norm=cols(L1_cond_g_norm), w_qkv=L1_cond_W_qkv, g_q=L1_cond_g_q, g_k=L1_cond_g_k,
        w_out=L1_cond_W_out, wall=flat(np.concatenate([rows(np.asarray(L2_cond_coupling).T), rows(L3_cond_W_hh)], axis=1)),
        bias2=cols(L2_cond_bias), w_ih=L3_cond_W_ih, b_ih=cols(L3_cond_b_ih), b_hh=cols(L3_cond_b_hh))
    arrays = {n: flat(v) for n, v in arrays.items()}
    nc = bacc.Bacc("TRN2", target_bir_lowering=False, num_devices=1)
    aps = {n: nc.dram_tensor("in_" + n, v.shape, F32, kind="ExternalInput").ap() for n, v in arrays.items()}
    aps["x1"] = nc.dram_tensor("x1_scratch", (B, P, 2 * SEQ_A), F32).ap()
    aps["out"] = nc.dram_tensor("out_y", (P, CHUNKS, C * CH * B), F32, kind="ExternalOutput").ap()
    build(nc, aps)
    got = launch(nc, [{"in_" + n: v for n, v in arrays.items()}], core_ids=[0]).results[0]["out_y"]
    return flat(np.asarray(got).reshape(P, CHUNKS, C, CH, B).transpose(4, 1, 3, 2, 0).reshape(B, T, D))
```

```python
from contextlib import ExitStack

import concourse.bass as bass
from concourse import mybir
ALU = mybir.AluOpType
ACT = mybir.ActivationFunctionType
F32 = mybir.dt.float32
F16 = mybir.dt.float16

P = 128
B = 8
T = 256
D = 512
C = D // P
CB = C * B
STEPS = 8
CH = 4
BODIES = T // STEPS
CHUNKS = T // CH
SC = 64.0

DT, EPSILON, ALPHA, BETA, CLAMP = 0.01, 0.08, 0.7, 0.8, 20.0
SHIFT = ALPHA / BETA
A_Q = [DT / 2, DT / 2, DT, DT / 6]


def recurrences(nc, sb, sem, psum, X, Wc, Wh, Wi, vec, out):
    bank_L2, bank_R, bank_N, bank_Z, bank_G = psum[0], psum[1], psum[2], psum[3], psum[4:6]
    ps2 = bank_L2[:, 0:2 * CB].rearrange("p (w c b) -> p w c b", w=2, c=C)
    gate_ps = [x[:, 0:2 * CB].rearrange("p (w c b) -> p w c b", w=2, c=C) for x in (bank_R, bank_N, bank_Z)]
    NG = 3 * C
    GU = NG // CH
    gi_ps = [x[:, 0:GU * 2 * CH * B].rearrange("p (g w n) -> p g w n", g=GU, w=2) for x in bank_G]

    st = lambda name: sb(name, [P, C, B], F32)
    q = [st(f"q{s + 1}") for s in range(4)]
    q_next, q_scaled = st("q_next"), st("q_scaled")
    p = [st(f"p{s + 1}") for s in range(4)]
    p_next = st("p_next")
    tanh32, cube, square, base, known, with_lo, pull = (st(x) for x in ("tanh32", "cube", "square", "base", "known", "with_lo", "pull"))
    q_third, p_third, q_sum, p_sum, q_avg, p_avg = (st(x) for x in ("q_third", "p_third", "q_sum", "p_sum", "q_avg", "p_avg"))
    drive_p = [st(f"drive_p{k}") for k in range(2)]
    rest = [st(f"rest{k}") for k in range(2)]
    thl = sb("tanh_parts", [P, C, 2, B], F16)
    hhl = sb("h_parts", [P, C, 2, B], F16)
    h, cand, tr, tz, r_pre, z_pre, r_lo, z_lo, n_lo, hn, rhn, n_pre, h_n, zh = (
        st(x) for x in ("h", "cand", "tanh_r", "tanh_z", "r_pre", "z_pre", "r_lo", "z_lo", "n_lo", "hn", "rhn", "n_pre", "h_minus_n", "zh"))
    bhn = st("b_hn")
    xr = [sb(f"x_chunk{k}", [P, C, CH, B], F32) for k in range(2)]
    dr = [sb(f"drive{k}", [P, C, CH, B], F32) for k in range(2)]
    x2 = [sb(f"x2_{k}", [P, C, CH, B], F32) for k in range(2)]
    x2p = [sb(f"x2_parts{k}", [P, C, 2, CH * B], F16) for k in range(2)]
    gi = [sb(f"gi{k}", [P, NG, CH, B], F32) for k in range(2)]
    yo = [sb(f"y{k}", [P, C, CH, B], F32) for k in range(2)]
    drive_bias = sb("drive_bias", [P, C, CH, B], F32)

    names = """q_ready q0_ready q_scaled_ready p_ready p0_ready tanh_hi tanh32_ready tanh_lo square_ready cube_ready base_ready
        known_ready with_lo_ready pull_ready q_third_ready p_third_ready  c2_done
        drive_p_ready rest_ready q_sum_ready p_sum_ready q_avg_ready p_avg_ready
        x_chunk_ready drive_ready x2_ready x2_hi_ready x2_parts_ready y_ready y_stored0 y_stored1
        r_done n_done z_done gi_done gi_biased gi_ready
        r_lo_ready r_pre_ready n_lo_ready hn_ready rhn_ready n_pre_ready z_lo_ready z_pre_ready zh_ready
        tr_ready cand_ready tz_ready h_n_ready h_ready h_hi_ready h_lo_ready p_raw_ready init_done""".split()
    S = {n: sem(n) for n in names}

    def wait(e, name, value):
        if isinstance(value, int) and value <= 0:
            return
        e.wait_ge(S[name], value)

    flat = lambda a: a[:].rearrange("p c b -> p (c b)")

    def l2_low(e):
        for c in range(C):
            for k in range(C):
                e.matmul(ps2[:, 0, c, :], Wc[1][:, k, c * P:(c + 1) * P], thl[:, k, 0, :],
                         start=(c == 0 and k == 0), stop=False, skip_group_check=True)

    def l2_high(e):
        for c in range(C):
            for k in range(C):
                mm = e.matmul(ps2[:, :, c, :], Wc[0][:, k, c * P:(c + 1) * P], thl[:, k, :, :],
                              start=False, stop=(c == C - 1 and k == C - 1), skip_group_check=True)
        return mm

    def l3_products(e, u, first, last):
        for x in range(first, last):
            gate, y = divmod(x, 2 * C * C)
            part, y = divmod(y, C * C)
            c, k = divmod(y, C)
            col = (0, 2, 1)[gate] * D + c * P
            if x == 0:
                wait(e, "h_hi_ready", u + 1)
            if x == C * C:
                wait(e, "h_lo_ready", u + 1)
            if part == 0:
                mm = e.matmul(gate_ps[gate][:, 0, c, :], Wh[1][:, k, col:col + P], hhl[:, k, 0, :],
                              start=(y == 0), stop=False, skip_group_check=True)
            else:
                mm = e.matmul(gate_ps[gate][:, :, c, :], Wh[0][:, k, col:col + P], hhl[:, k, :, :],
                              start=False, stop=(y == C * C - 1), skip_group_check=True)
            if part == 1 and y == C * C - 1:
                mm.then_inc(S[("r_done", "n_done", "z_done")[gate]], 1)

    def gi_products(e, v, kappa, par, first, last):
        for x in range(first, last):
            g, y = divmod(x, 2 * C)
            k, part = divmod(y, 2)
            gg, bank = g, kappa % 2
            g += kappa * GU
            if x == 0:
                wait(e, "gi_ready", v - 1)
            if x == 0 and kappa == 0:
                wait(e, "x2_parts_ready", v + CH)
            if part == 0:
                mm = e.matmul(gi_ps[bank][:, gg, :, :], Wi[0][:, k, g * P:(g + 1) * P], x2p[par][:, k, :, :],
                              start=(gg == 0 and k == 0), stop=False, skip_group_check=True)
            else:
                mm = e.matmul(gi_ps[bank][:, gg, 0, :], Wi[1][:, k, g * P:(g + 1) * P], x2p[par][:, k, 0, :],
                              start=False, stop=(k == C - 1), skip_group_check=True)
        if last == 2 * C * GU:
            mm.then_inc(S["gi_done"], 1)

    def tensor_step(e, i, tau, l2, l3, gi_now, gi_before):
        t, u, v = i * STEPS + tau, (i - 1) * STEPS + tau, i * STEPS + tau - CH
        kappa, par = tau % CH, (tau // CH + 1) % 2
        for s in range(4):
            n = t * 4 + s
            if l2:
                wait(e, "tanh_hi", n + 1)
                l2_low(e)
            if l2:
                wait(e, "tanh_lo", n + 1)
                l2_high(e).then_inc(S["c2_done"], 1)
            if l3 and s < 3:
                l3_products(e, u, 32 * s, 32 * s + 32)
        if gi_now:
            gi_products(e, v, kappa, par, 0, 2 * C * GU)

    def tanh_of(e, n, src, src_sq, sq_sem, sq_value):
        wait(e, "q_ready", n + 1)
        e.activation(thl[:, :, 0, :], src[:], ACT.Tanh).then_inc(S["tanh_hi"], 1)
        e.activation(tanh32[:], src[:], ACT.Tanh).then_inc(S["tanh32_ready"], 1)
        wait(e, sq_sem, sq_value)
        e.activation(square[:], src_sq[:], ACT.Square).then_inc(S["square_ready"], 1)

    def scale_q(e):
        e.activation(q_scaled[:], q[0][:], ACT.Copy, scale=1 + A_Q[0]).then_inc(S["q_scaled_ready"], 1)

    def scalar_step(e, i, tau, l2, l3, gi_before):
        t, u, v = i * STEPS + tau, (i - 1) * STEPS + tau, i * STEPS + tau - CH
        half = tau // CH
        for s in range(4):
            n = t * 4 + s
            if s == 0 and gi_before:
                wait(e, "gi_done", v)
                k0 = (tau - 1) % CH
                for gg in range(GU):
                    g = k0 * GU + gg
                    ins = e.activation(gi[((tau - 1) // CH + 1) % 2][:, g, :, :].rearrange("p t b -> p (t b)"),
                                       gi_ps[k0 % 2][:, gg, 0, :], ACT.Identity, bias=vec["b_gates"][:, g:g + 1], scale=1 / SC)
                ins.then_inc(S["gi_biased"], 1)
            if s == 1 and l2 and tau % CH == 2:
                wait(e, "x2_ready", t - 2)
                e.activation(xr[(half + 1) % 2][:].rearrange("p c t b -> p c (t b)"),
                             X[:, :, bass.ds((i * 2 + (half + 1)) * CH * B, CH * B)], ACT.Copy).then_inc(S["x_chunk_ready"], 1)
            if s == 2 and l2:
                wait(e, "q_sum_ready", t + 1)
                e.activation(q_avg[:], q_sum[:], ACT.Copy, scale=1 / 3).then_inc(S["q_avg_ready"], 1)
                wait(e, "p_sum_ready", t + 1)
                e.activation(p_avg[:], p_sum[:], ACT.Copy, scale=1 / 3).then_inc(S["p_avg_ready"], 1)
            if s == 1 and l3:
                wait(e, "r_pre_ready", u + 1)
                e.activation(tr[:], r_pre[:], ACT.Tanh, scale=0.5).then_inc(S["tr_ready"], 1)
            if s == 3 and l3:
                wait(e, "n_pre_ready", u + 1)
                e.activation(cand[:], n_pre[:], ACT.Tanh).then_inc(S["cand_ready"], 1)
                wait(e, "z_pre_ready", u + 1)
                e.activation(tz[:], z_pre[:], ACT.Tanh, scale=0.5).then_inc(S["tz_ready"], 1)
            if l2:
                if s < 3:
                    tanh_of(e, n + 1, q[s + 1], q[s + 1], "q_ready", n + 2)
                else:
                    tanh_of(e, n + 1, q_next, q[0], "q0_ready", t + 2)
        if l3:
            wait(e, "h_ready", u + 2)
            e.activation(hhl[:, :, 0, :], h[:], ACT.Copy).then_inc(S["h_hi_ready"], 1)
        if l2:
            scale_q(e)

    def gate_sum(e, gate, u, gpar, kappa, part):
        lo, full, src = ((r_lo, r_pre, "r"), (n_lo, hn, "n"), (z_lo, z_pre, "z"))[gate]
        if part == 0:
            other = bhn[:] if gate == 1 else gi[gpar][:, (0 if gate == 0 else C):(C if gate == 0 else 2 * C), kappa, :]
            if gate == 0 and kappa == 0:
                wait(e, "gi_ready", u + CH)
            wait(e, src + "_done", u + 1)
            e.scalar_tensor_tensor(out=lo[:], in0=gate_ps[gate][:, 1, :, :], scalar=1 / SC, in1=other,
                                   op0=ALU.mult, op1=ALU.add).then_inc(S[src + "_lo_ready"], 1)
        else:
            wait(e, src + "_lo_ready", u + 1)
            e.scalar_tensor_tensor(out=full[:], in0=gate_ps[gate][:, 0, :, :], scalar=1 / SC, in1=lo[:],
                                   op0=ALU.mult, op1=ALU.add).then_inc(S["hn_ready" if gate == 1 else src + "_pre_ready"], 1)

    def vector_step(e, i, tau, l2, l3, gi_before):
        t, u, v = i * STEPS + tau, (i - 1) * STEPS + tau, i * STEPS + tau - CH
        kappa, gpar = tau % CH, (tau // CH) % 2
        stt = e.scalar_tensor_tensor

        for s in range(4):
            n = t * 4 + s
            a = A_Q[s]
            if l2:
                wait(e, "square_ready", n + 1)
                stt(out=flat(cube), in0=flat(square), scalar=-1 / 3, in1=flat(q[s]), op0=ALU.mult, op1=ALU.mult).then_inc(S["cube_ready"], 1)
                wait(e, "p_ready" if s else "p0_ready", t * 3 + s if s else t + 1)
                stt(out=flat(pull), in0=flat(p[s]), scalar=-BETA, in1=flat(q[s]), op0=ALU.mult, op1=ALU.add).then_inc(S["pull_ready"], 1)
            if l3 and s:
                gate_sum(e, s - 1, u, gpar, kappa, 0)
            if l2:
                if s == 0:
                    wait(e, "q_scaled_ready", t + 1)
                    wait(e, "drive_p_ready", n + 1)
                    src, other = drive_p[0], q_scaled
                else:
                    if s == 3:
                        wait(e, "q_third_ready", t + 1)
                    wait(e, "rest_ready", t * 3 + s)
                    src, other = rest[s % 2], (q_third if s == 3 else q[0])
                stt(out=flat(base), in0=flat(src), scalar=a, in1=flat(other), op0=ALU.mult, op1=ALU.add).then_inc(S["base_ready"], 1)
            if s == 0 and l3:
                wait(e, "h_hi_ready", u + 1)
                e.tensor_tensor(hhl[:, :, 1, :], h[:], hhl[:, :, 0, :], ALU.subtract).then_inc(S["h_lo_ready"], 1)
            if l2 and s in (1, 2):
                wait(e, "pull_ready", n + 1)
                stt(out=flat(p[s + 1]), in0=flat(pull), scalar=A_Q[s] * EPSILON, in1=flat(p[0]),
                    op0=ALU.mult, op1=ALU.add).then_inc(S["p_ready"], 1)
            if l2:
                wait(e, "base_ready", n + 1)
                stt(out=flat(known), in0=flat(cube), scalar=a, in1=flat(base), op0=ALU.mult, op1=ALU.add).then_inc(S["known_ready"], 1)
            if l2 and s == 0:
                wait(e, "pull_ready", n + 1)
                stt(out=flat(p[s + 1]), in0=flat(pull), scalar=A_Q[s] * EPSILON, in1=flat(p[0]),
                    op0=ALU.mult, op1=ALU.add).then_inc(S["p_ready"], 1)
            if l3 and s:
                gate_sum(e, s - 1, u, gpar, kappa, 1)
            if l2:
                wait(e, "c2_done", n + 1)
                wait(e, "known_ready", n + 1)
                stt(out=with_lo[:], in0=ps2[:, 1, :, :], scalar=a / SC, in1=known[:], op0=ALU.mult, op1=ALU.add).then_inc(S["with_lo_ready"], 1)
                if s == 3:
                    wait(e, "p_avg_ready", t + 1)
                    stt(out=flat(p_third), in0=flat(p[3]), scalar=1 / 3, in1=flat(p_avg), op0=ALU.mult, op1=ALU.add).then_inc(S["p_third_ready"], 1)
                wait(e, "with_lo_ready", n + 1)
                nxt = q[s + 1] if s < 3 else q_next
                stt(out=nxt[:], in0=ps2[:, 0, :, :], scalar=a / SC, in1=with_lo[:], op0=ALU.mult, op1=ALU.add).then_inc(S["q_ready"], 1)
            if s == 0 and gi_before:
                wait(e, "gi_biased", v)
                k0 = (tau - 1) % CH
                dst = gi[((tau - 1) // CH + 1) % 2][:, k0 * GU:(k0 + 1) * GU, :, :].rearrange("p g t b -> p g (t b)")
                stt(out=dst, in0=gi_ps[k0 % 2][:, :, 1, :], scalar=1 / SC, in1=dst,
                    op0=ALU.mult, op1=ALU.add).then_inc(S["gi_ready"], 1)
            if s == 2 and l3:
                wait(e, "tr_ready", u + 1)
                wait(e, "hn_ready", u + 1)
                stt(out=flat(rhn), in0=flat(tr), scalar=1.0, in1=flat(hn), op0=ALU.add, op1=ALU.mult).then_inc(S["rhn_ready"], 1)
            if s == 2 and l2:
                wait(e, "q_avg_ready", t + 1)
                wait(e, "q_ready", n + 2)
                stt(out=flat(q_third), in0=flat(q[3]), scalar=1 / 3, in1=flat(q_avg), op0=ALU.mult, op1=ALU.add).then_inc(S["q_third_ready"], 1)
            if s == 2 and l3:
                wait(e, "rhn_ready", u + 1)
                stt(out=n_pre[:], in0=rhn[:], scalar=0.5, in1=gi[gpar][:, 2 * C:3 * C, kappa, :], op0=ALU.mult, op1=ALU.add).then_inc(S["n_pre_ready"], 1)
            if s == 3 and l2:
                wait(e, "p_third_ready", t + 1)
                stt(out=flat(p_next), in0=flat(pull), scalar=DT / 6 * EPSILON, in1=flat(p_third),
                    op0=ALU.mult, op1=ALU.add).then_inc(S["p_raw_ready"], 1)
            if s == 3 and l3:
                wait(e, "tz_ready", u + 1)
                wait(e, "h_n_ready", u + 1)
                stt(out=flat(zh), in0=flat(tz), scalar=1.0, in1=flat(h_n), op0=ALU.add, op1=ALU.mult).then_inc(S["zh_ready"], 1)
            if s == 3 and l2:
                wait(e, "q_ready", n + 2)
                e.tensor_scalar(flat(q[0]), flat(q_next), CLAMP, -CLAMP, ALU.min, ALU.max).then_inc(S["q0_ready"], 1)
            if s == 3 and l2:
                wait(e, "p_raw_ready", t + 1)
                e.tensor_scalar(flat(p[0]), flat(p_next), CLAMP - SHIFT, -CLAMP - SHIFT, ALU.min, ALU.max).then_inc(S["p0_ready"], 1)
            if s == 3 and l3:
                wait(e, "zh_ready", u + 1)
                stt(out=flat(h), in0=flat(zh), scalar=0.5, in1=flat(cand), op0=ALU.mult, op1=ALU.add).then_inc(S["h_ready"], 1)
            if l2:
                wait(e, "tanh32_ready", n + 2)
                e.tensor_tensor(thl[:, :, 1, :], tanh32[:], thl[:, :, 0, :], ALU.subtract).then_inc(S["tanh_lo"], 1)

    def gpsimd_step(e, i, tau, l2, l3):
        t, u = i * STEPS + tau, (i - 1) * STEPS + tau
        half, kappa = tau // CH, tau % CH
        tt = e.tensor_tensor
        for s in range(4):
            n = t * 4 + s
            if l2 and s == 1:
                tt(flat(q_third_sum), flat(q[1]), flat(q[0]), ALU.subtract).then_inc(S["q_sum1"], 1)
                tt(flat(p_third_sum), flat(p[1]), flat(p[0]), ALU.subtract).then_inc(S["p_sum1"], 1)
                if kappa == 2:
                    wait(e, "x_chunk_ready", i * 2 + (half + 2))
                    o = (half + 1) % 2
                    tt(dr[o][:].rearrange("p c t b -> p (c t b)"), xr[o][:].rearrange("p c t b -> p (c t b)"),
                       drive_bias[:].rearrange("p c t b -> p (c t b)"), ALU.add).then_inc(S["drive_ready"], 1)
            if l2 and s == 2:
                wait(e, "q_sum1", t + 1)
                tt(flat(q_sum2), flat(q_third_sum), flat(q[2]), ALU.add).then_inc(S["q_sum2s"], 1)
                wait(e, "p_sum1", t + 1)
                tt(flat(p_sum2), flat(p_third_sum), flat(p[2]), ALU.add).then_inc(S["p_sum2s"], 1)
                wait(e, "q_sum2s", t + 1)
                tt(flat(q_sum), flat(q_sum2), flat(q[2]), ALU.add).then_inc(S["q_sum_ready"], 1)
                wait(e, "p_sum2s", t + 1)
                tt(flat(p_sum), flat(p_sum2), flat(p[2]), ALU.add).then_inc(S["p_sum_ready"], 1)
            if l3 and s == 3:
                wait(e, "cand_ready", u + 1)
                tt(flat(h_n), flat(h), flat(cand), ALU.subtract).then_inc(S["h_n_ready"], 1)
            if l2:
                if s < 3:
                    wait(e, "p_ready", t * 3 + s + 1)
                    d = dr[half][:, :, kappa, :]
                else:
                    wait(e, "p0_ready", t + 2)
                    d = dr[((tau + 1) // CH) % 2][:, :, (tau + 1) % CH, :]
                    if kappa == CH - 1:
                        wait(e, "drive_ready", i * 2 + (half + 2))
                tt(drive_p[(s + 1) % 2][:], d, p[(s + 1) % 4][:], ALU.subtract).then_inc(S["drive_p_ready"], 1)
                if s < 3:
                    wait(e, "q_ready", n + 2)
                    wait(e, "drive_p_ready", n + 2)
                    tt(flat(rest[(s + 1) % 2]), flat(drive_p[(s + 1) % 2]), flat(q[s + 1]), ALU.add).then_inc(S["rest_ready"], 1)
        if l3:
            wait(e, "h_ready", u + 2)
            if kappa == 0:
                wait(e, f"y_stored{half}", i * 16)
            tt(yo[half][:, :, kappa, :], x2[half][:, :, kappa, :], h[:], ALU.add).then_inc(S["y_ready"], 1)
        if l2:
            if l3:
                wait(e, "y_ready", u + 1)
            tt(x2[half][:, :, kappa, :], xr[half][:, :, kappa, :], q[0][:], ALU.add).then_inc(S["x2_ready"], 1)
            hi = x2p[half][:, :, 0, kappa * B:(kappa + 1) * B]
            tt(hi, xr[half][:, :, kappa, :], q[0][:], ALU.add).then_inc(S["x2_hi_ready"], 1)
            wait(e, "x2_hi_ready", t + 1)
            tt(x2p[half][:, :, 1, kappa * B:(kappa + 1) * B], x2[half][:, :, kappa, :], hi, ALU.subtract).then_inc(S["x2_parts_ready"], 1)

    q_third_sum, p_third_sum, q_sum2, p_sum2 = (st(x) for x in ("q_sum1_", "p_sum1_", "q_sum2_", "p_sum2_"))
    for x in ("q_sum1", "p_sum1", "q_sum2s", "p_sum2s"):
        S[x] = sem(x)

    def vector_start(e):
        cond = vec["cond_t"]
        e.tensor_copy(flat(q[0]), cond).then_inc(S["q0_ready"], 1)
        e.tensor_copy(flat(q_next), cond).then_inc(S["q_ready"], 1)
        e.tensor_copy(flat(h), cond).then_inc(S["h_ready"], 1)
        e.tensor_scalar(flat(p[0]), cond, -SHIFT, None, ALU.add).then_inc(S["p0_ready"], 1)
        for c in range(C):
            e.memset(bhn[:, c, :], 0.0)
        for c in range(C):
            e.memset(drive_bias[:, c, :, :], -SHIFT)
        for k in range(2):
            e.memset(yo[k][:], 0.0).then_inc(S[f"y_stored{k}"], 16)
        e.memset(X[:, :, T * B:(T + CH) * B], 0.0).then_inc(S["init_done"], 1)
        wait(e, "init_done", 1)
        for c in range(C):
            e.tensor_scalar(bhn[:, c, :], bhn[:, c, :], vec["b_hn"][:, c:c + 1], None, ALU.add)
        for c in range(C):
            w = drive_bias[:, c, :, :].rearrange("p t b -> p (t b)")
            ins = e.tensor_scalar(w, w, vec["bias2"][:, c:c + 1], None, ALU.add)
        ins.then_inc(S["init_done"], 1)
        wait(e, "init_done", 2)

    def vector_first_lo(e):
        wait(e, "tanh32_ready", 1)
        e.tensor_tensor(thl[:, :, 1, :], tanh32[:], thl[:, :, 0, :], ALU.subtract).then_inc(S["tanh_lo"], 1)

    def scalar_start(e):
        e.activation(xr[0][:].rearrange("p c t b -> p c (t b)"), X[:, :, 0:CH * B], ACT.Copy).then_inc(S["x_chunk_ready"], 1)
        tanh_of(e, 0, q_next, q[0], "q0_ready", 1)
        scale_q(e)
        wait(e, "h_ready", 1)
        e.activation(hhl[:, :, 0, :], h[:], ACT.Copy).then_inc(S["h_hi_ready"], 1)

    def gpsimd_start(e):
        wait(e, "x_chunk_ready", 1)
        wait(e, "init_done", 2)
        tt = e.tensor_tensor
        tt(dr[0][:].rearrange("p c t b -> p (c t b)"), xr[0][:].rearrange("p c t b -> p (c t b)"),
           drive_bias[:].rearrange("p c t b -> p (c t b)"), ALU.add).then_inc(S["drive_ready"], 1)
        wait(e, "drive_ready", 1)
        wait(e, "p0_ready", 1)
        tt(drive_p[0][:], dr[0][:, :, 0, :], p[0][:], ALU.subtract).then_inc(S["drive_p_ready"], 1)

    def run(e, step):
        step(e, 0, "first")
        with e.Fori(1, BODIES) as i:
            step(e, i, "loop")
        step(e, BODIES, "last")

    def has(which, tau):
        l2 = which != "last"
        l3 = which != "first"
        gi_now = which == "loop" or (which == "first" and tau >= CH) or (which == "last" and tau < CH)
        gi_before = which == "loop" or (which == "first" and tau > CH) or (which == "last" and tau <= CH)
        return l2, l3, gi_now, gi_before

    def tensor(e):
        def body(e, i, which):
            for tau in range(STEPS):
                tensor_step(e, i, tau, *has(which, tau))
        run(e, body)

    def scalar(e):
        scalar_start(e)
        def body(e, i, which):
            for tau in range(STEPS):
                l2, l3, _, before = has(which, tau)
                scalar_step(e, i, tau, l2, l3, before)
        run(e, body)

    def vector(e):
        vector_first_lo(e)
        def body(e, i, which):
            for tau in range(STEPS):
                l2, l3, _, before = has(which, tau)
                vector_step(e, i, tau, l2, l3, before)
        run(e, body)

    def gpsimd(e):
        gpsimd_start(e)
        def body(e, i, which):
            for tau in range(STEPS):
                l2, l3, _, _ = has(which, tau)
                gpsimd_step(e, i, tau, l2, l3)
        run(e, body)

    def sync(e):
        def store(e, jj, par):
            at = jj if isinstance(jj, int) else e.snap(jj)
            wait(e, "y_ready", jj * CH + CH)
            e.dma_start(out[:, bass.ds(at, 1), :],
                        yo[par][:].rearrange("p c t b -> p (c t b)").rearrange("p (o n) -> p o n", o=1)).then_inc(S[f"y_stored{par}"], 16)
        with e.Fori(1, BODIES) as i:
            store(e, (i - 1) * 2, 0)
            store(e, (i - 1) * 2 + 1, 1)
        store(e, (BODIES - 1) * 2, 0)
        store(e, (BODIES - 1) * 2 + 1, 1)
        for k in range(2):
            wait(e, f"y_stored{k}", 16 * (BODIES + 1))

    return dict(tensor=tensor, scalar=scalar, vector=vector, gpsimd=gpsimd, sync=sync, vector_start=vector_start, S=S)


SEQ_A, HEADS_A, DIM_A = 512, 8, 256
SEQ_B, HEADS_B, DIM_B = 256, 16, 512
DH = 32
VW = 2 * DH
NEG = -1e30
ROWS = 3 * DH
MAX_SCALE = 64.0
WALL = C * (D + 3 * D)
ARENA = 34816
UNIT = WALL // 8
OUT_AT, ADD_AT = 3, 5


def per_batch(b, per, plus):
    i, k = b
    return i * (2 * per) + (k * per + plus)


def parity(b):
    return b[1] % 2


def loads(b):
    return (b[0] + b[1] // 2) * 16 + 16


def wait_pos(e, sem, value):
    if isinstance(value, int) and value <= 0:
        return
    e.wait_ge(sem, value)


def attention_core(name, sem, psum, heads, keys, QK, V, prob, mx, mrow, ident, ctx, den, mask_bias, guard_col, keep_col):
    per = 512 // keys
    tiles = heads * (keys // 128) // per
    bank_s, bank_t, bank_o = psum[2:4], psum[4:6], psum[6:8]
    half = tiles // 2
    kb = keys // 128
    names = """score0_done score1_done score0_free score1_free maxT_row packed
        weights_scores exp_done pv_done pair_free den_ready inv_ready rec_ready""".split()
    S = {n: sem(f"{name}_{n}") for n in names}
    LAG = 2
    EXP0, PV0, FREE0 = 2, 4, 2

    first = tiles // 2 if keys == 512 else tiles * 3 // 4
    after = {x: [] for x in range(tiles)}
    for j in range(tiles):
        after[first + (tiles - first) * j // tiles].append(j)

    def block(x):
        return (x * per // (keys // 128), x * per % (keys // 128))

    class Core:
        sems = S

        @staticmethod
        def prime(e):
            e.nop().then_inc(S["exp_done"], EXP0)
            e.nop().then_inc(S["pv_done"], PV0)
            e.nop().then_inc(S["pair_free"], FREE0)

        @staticmethod
        def score_tile(e, b, par, j):
            s = j % 2
            wait_pos(e, S[f"score{s}_free"], per_batch(b, half + (s == 0), j // 2))
            if j == 0:
                e.wait_ge(S["packed"], per_batch(b, 16 * 24, 16 * 24))
            h, blk = block(j)
            for y in range(per):
                mm = e.matmul(bank_s[s][:, y * keys:(y + 1) * keys], QK[par][0][0:ROWS, h, (blk + y) * 128:(blk + y + 1) * 128],
                              QK[par][1][0:ROWS, h, :], start=True, stop=True)
            mm.then_inc(S[f"score{s}_done"], 1)

        @staticmethod
        def max_tile(e, b, j):
            s = j % 2
            e.wait_ge(S[f"score{s}_done"], per_batch(b, half + (s == 0), j // 2 + 1))
            e.tensor_reduce(mx[:, j * per:(j + 1) * per], bank_s[s][:, :].rearrange("p (y k) -> p y k", y=per),
                            mybir.AxisListType.X, ALU.max).then_inc(S[f"score{s}_free"], 1)

        @staticmethod
        def max_rows(e, b):
            wait_pos(e, S["score0_free"], per_batch(b, half + 1, half))
            e.wait_ge(S["score1_free"], per_batch(b, half, half))
            e.transpose(bank_s[0][0:32, 0:128], mx[:, :], ident[:, :]).then_inc(S["score0_done"], 1)

        @staticmethod
        def shift_rows(e, b):
            e.wait_ge(S["score0_done"], per_batch(b, half + 1, half + 1))
            wait_pos(e, S["maxT_row"], per_batch(b, 16, 0))
            e.activation(mrow[:, :], bank_s[0][0:32, 0:128], ACT.Copy, scale=-1 / MAX_SCALE).then_inc(S["score0_free"], 1)

        @staticmethod
        def move_shift(e, b, par):
            e.wait_ge(S["score0_free"], per_batch(b, half + 1, half + 1))
            e.dma_start(QK[par][0][ROWS:ROWS + 1, :, :].rearrange("p h q -> p (h q)"), mrow[:, :]).then_inc(S["maxT_row"], 16)

        @staticmethod
        def weight_tile(e, b, par, x):
            if x == 0:
                e.wait_ge(S["maxT_row"], per_batch(b, 16, 16))
            e.wait_ge(S["exp_done"], per_batch(b, tiles, x - 1 + EXP0))
            h, blk = block(x)
            for y in range(per):
                mm = e.matmul(bank_t[x % 2][:, y * keys:(y + 1) * keys], QK[par][1][0:ROWS + 1, h, (blk + y) * 128:(blk + y + 1) * 128],
                              QK[par][0][0:ROWS + 1, h, :], start=True, stop=True)
            mm.then_inc(S["weights_scores"], 1)

        @staticmethod
        def exp_tile(e, b, x, par):
            e.wait_ge(S["weights_scores"], per_batch(b, tiles, x + 1))
            e.wait_ge(S["pv_done"], per_batch(b, tiles, x - 3 + PV0))
            bias = {} if mask_bias is None else dict(bias=mask_bias[par][:, x % 4:x % 4 + 1])
            e.activation(prob[x % 4][:, :], bank_t[x % 2][:, :], ACT.Exp, scale=DH ** -0.5, **bias).then_inc(S["exp_done"], 1)

        @staticmethod
        def pv_tile(e, b, par, x):
            h, blk = block(x)
            pair, z = divmod(h, 2)
            if blk == 0 and z == 0:
                e.wait_ge(S["pair_free"], per_batch(b, heads // 2, pair - 1 + FREE0))
            e.wait_ge(S["exp_done"], per_batch(b, tiles, x + 1 + EXP0))
            for y in range(per):
                for a in range(kb):
                    at = (z * kb + a) * VW
                    mm = e.matmul(bank_o[pair % 2][:, at:at + VW], prob[x % 4][:, y * keys + a * 128:y * keys + (a + 1) * 128],
                                  V[par][:, blk + y, h, :], start=(z == 0 and blk + y == 0 and a == 0), stop=(blk + y == kb - 1),
                                  skip_group_check=True)
            mm.then_inc(S["pv_done"], 1)

        @staticmethod
        def divide(e, b, pair):
            e.wait_ge(S["pv_done"], per_batch(b, tiles, (pair + 1) * tiles * 2 // heads + PV0))
            sums = bank_o[pair % 2][:, 0:2 * kb * VW].rearrange("p (z a d) -> p z a d", z=2, d=VW)
            rec = den[:, 0:2 * kb].rearrange("p (z a o) -> p z a o", z=2, o=1)
            n = per_batch(b, heads // 2, pair + 1)
            e.wait_ge(S["pair_free"], per_batch(b, heads // 2, pair + FREE0))
            if guard_col is None:
                e.reciprocal(rec, sums[:, :, :, DH:DH + 1]).then_inc(S["rec_ready"], 1)
            else:
                col = lambda v: v[parity(b)][:, :].rearrange("p (o a q) -> p o a q", o=1, q=1).to_broadcast([P, 2, kb, 1])
                e.tensor_tensor(rec, sums[:, :, :, DH:DH + 1], col(guard_col), ALU.add).then_inc(S["den_ready"], 1)
                e.wait_ge(S["den_ready"], n)
                e.reciprocal(den[:, 0:2 * kb], den[:, 0:2 * kb]).then_inc(S["inv_ready"], 1)
                e.wait_ge(S["inv_ready"], n)
                e.tensor_tensor(rec, rec, col(keep_col), ALU.mult).then_inc(S["rec_ready"], 1)
            e.wait_ge(S["rec_ready"], n)
            e.tensor_tensor(ctx[:, :, 2 * pair:2 * pair + 2, :].rearrange("p a z d -> p z a d"), sums[:, :, :, 0:DH],
                            rec.to_broadcast([P, 2, kb, DH]), ALU.mult).then_inc(S["pair_free"], 1)

    Core.EXP0, Core.PV0, Core.FREE0 = EXP0, PV0, FREE0
    Core.tiles, Core.after, Core.LAG, Core.pairs = tiles, after, LAG, heads // 2
    return Core


def pack(e, core, b, QKp, parts, heads):
    qh, ql, kh, kl = parts
    for side, blocks in ((0, (qh, qh, ql)), (1, (kh, kl, kh))):
        for row, src in enumerate(blocks):
            for j in range(4):
                dst = QKp[side][row * DH:(row + 1) * DH, :, :].rearrange("p (g j) q -> p g j q", j=4)[:, :, j, :]
                e.dma_start(dst, src[j * DH:(j + 1) * DH, :, :]).then_inc(core.sems["packed"], 16)


def build(nc, a):
    with ExitStack() as stack:
        def sb(name, shape, dt):
            return stack.enter_context(nc.sbuf_tensor("sb_" + name, shape, dt))

        def sem(name):
            return stack.enter_context(nc.semaphore(name))

        psum = [stack.enter_context(nc.psum_tensor(f"bank{k}", [P, 512], F32)) for k in range(8)]

        X = sb("X", [P, C, (T + CH) * B], F32)
        w_parts = [sb(f"w_parts{k}", [P, WALL], F16) for k in range(2)]
        arena = sb("arena", [P, ARENA], F32)
        ident = sb("ident", [P, P], F32)
        cond_t = sb("cond_t", [P, C * B], F32)
        ssq = sb("ssq", [P, 2 * B], F32)
        rstd = sb("rstd", [P, 2 * B], F32)
        head_ones = sb("head_ones", [P, P], F32)
        mx = sb("mx", [P, 32], F32)
        mrow = sb("mrow", [32, P], F16)
        mask_col = [sb(f"mask_col{k}", [P, 4], F32) for k in range(2)]
        mask_bias = [sb(f"mask_bias{k}", [P, 4], F32) for k in range(2)]
        guard_col = [sb(f"guard_col{k}", [P, 4], F32) for k in range(2)]
        keep_col = [sb(f"keep_col{k}", [P, 4], F32) for k in range(2)]
        v_sum = sb("v_sum", [P, 2 * B], F32)
        den = sb("den", [P, 8], F32)
        g_q, g_k = sb("g_q", [P, 1], F32), sb("g_k", [P, 1], F32)
        g_norm = sb("g_norm", [P, C], F32)
        b_emb = sb("b_emb", [P, 2 * C], F32)
        eps = sb("eps", [P, 1], F32)
        mod = sb("mod", [P, 2 * C, B], F32)
        mod_b = [sb(f"mod_b{k}", [P, 2 * C], F32) for k in range(2)]
        bias2 = sb("bias2", [P, C], F32)
        b_ih, b_hh, b_gates = (sb(x, [P, 3 * C], F32) for x in ("b_ih", "b_hh", "b_gates"))

        def cut(at, shape, dt=F32):
            n = 1
            for x in shape:
                n *= x
            cols = n * (2 if dt is F16 else 4) // 4
            v = arena[:, at:at + cols]
            if dt is F16:
                v = v.bitcast(F16)
            names = "abc"[:len(shape)]
            if len(shape) > 1:
                v = v.rearrange(f"p ({' '.join(names)}) -> p {' '.join(names)}", **{m: s for m, s in zip(names, shape)})
            return v, at + cols

        x_flat = X[:, :, :].rearrange("p c n -> p (c n)")
        w_emb = x_flat[:, 0:4 * 1024].rearrange("p (k n) -> p k n", k=C)
        stage = [x_flat[:, 4096 + k * UNIT:4096 + (k + 1) * UNIT] for k in range(2)]

        at = 0
        xb, qk_a, v_a, prob_a, crow, irow = [], [], [], [], [], []
        for k in range(2):
            v, at = cut(at, (2, SEQ_A)); xb.append(v)
        xres, at = cut(at, (2, SEQ_A))
        wq, at = cut(at, (2, DIM_A))
        wo, at = cut(at, (2, DIM_A))
        parts_a = []
        for k in range(4):
            v, at = cut(at, (2, SEQ_A), F16); parts_a.append(v)
        for k in range(2):
            u, at = cut(at, (HEADS_A, SEQ_A), F16)
            v, at = cut(at, (HEADS_A, SEQ_A), F16)
            qk_a.append((u, v))
        for k in range(2):
            v, at = cut(at, (4, HEADS_A, VW)); v_a.append(v)
        for k in range(4):
            v, at = cut(at, (512,)); prob_a.append(v)
        for k in range(2):
            v, at = cut(at, (SEQ_A,)); crow.append(v)
            v, at = cut(at, (SEQ_A,)); irow.append(v)
        squares = []
        for k in range(2):
            v, at = cut(at, (SEQ_A,), F16); squares.append(v)
        ctx_a, at = cut(at, (2, SEQ_A))
        heads_a, at = cut(at, (4, HEADS_A, DH))
        assert at <= ARENA - 1540
        CA = attention_core("a", sem, psum, HEADS_A, SEQ_A, qk_a, v_a, prob_a, mx, mrow, ident, heads_a, den, mask_bias, guard_col, keep_col)

        A = {n: sem("a_" + n) for n in """weights_in ident_ready start_ready res_in pj0_done pj1_done pj0_free pj1_free
            q_hi_ready q_lo_ready k_masked row_ready row_scaled col_ready split_hi split_done v_ready
            bias_ready blended added res_used""".split()}
        for n in ("x_in", "mask_in", "stage_in"):
            A[n] = [sem(f"a_{n}{k}") for k in range(2)]

        at = 0
        wqkv, at = cut(at, (C, 3 * D))
        after_wqkv = at
        raw, at = cut(at, (8, SEQ_B))
        sq, at = cut(at, (4, 512))
        xnT, at = cut(at, (C, SEQ_B))
        xs, at = cut(at, (2, D))
        parts_b = []
        for k in range(4):
            v, at = cut(at, (4, SEQ_B), F16); parts_b.append(v)
        wout, at = cut(at, (C, D))
        x1, at = cut(at, (2, D))
        x1_res, at = cut(at, (2, D))
        qk_b, v_b, prob_b = [], [], []
        after_x1 = at
        for k in range(2):
            u, at = cut(at, (HEADS_B, SEQ_B), F16)
            v, at = cut(at, (HEADS_B, SEQ_B), F16)
            qk_b.append((u, v))
        for k in range(2):
            v, at = cut(at, (2, HEADS_B, VW)); v_b.append(v)
        for k in range(4):
            v, at = cut(at, (512,)); prob_b.append(v)
        ctx_b, at = cut(at, (C, SEQ_B))
        heads_b, at = cut(at, (2, HEADS_B, DH))
        assert at <= ARENA
        CB_ = attention_core("b", sem, psum, HEADS_B, SEQ_B, qk_b, v_b, prob_b, mx, mrow, ident, heads_b, den, None, None, None)
        Bs = {n: sem("b_" + n) for n in """weights_in start_ready emb_in emb_done mod0 mod_ready rstd0 rstd_ready xs_ready modb_ready
            pj0_done pj1_done pj0_free pj1_free sq_ready raw_ready root_ready half_ready norm_ready hi_ready lo_ready xn_ready v_ready turned res_in
            x_written x1_in wih_in wih_hi wih_done""".split()}

        c_at = [after_x1]

        def sbc(name, shape, dt):
            v, c_at[0] = cut(c_at[0], tuple(shape[1:]), dt)
            return v
        wih_parts = []
        at = after_wqkv
        for k in range(2):
            v, at = cut(at, (C, 3 * D), F16); wih_parts.append(v)
        assert at <= after_wqkv + 7168
        cw = [w_parts[k][:, 0:C * D].rearrange("p (k n) -> p k n", k=C) for k in range(2)]
        hw = [w_parts[k][:, C * D:WALL].rearrange("p (k n) -> p k n", k=C) for k in range(2)]
        R = recurrences(nc, sbc, sem, psum, X, cw, hw, wih_parts,
                        dict(cond_t=cond_t[:, :], b_gates=b_gates, b_hn=b_hh[:, 2 * C:3 * C], bias2=bias2), a["out"])
        assert c_at[0] <= ARENA

        block = stack.enter_context(nc.Block())

        def slots(e, body):
            body(e, (0, 0), False, True)
            with e.Fori(0, B // 2 - 1) as i:
                body(e, (i, 1), True, True)
                body(e, (i, 2), True, True)
            body(e, (B // 2 - 1, 1), True, False)

        def nxt(b):
            return (b[0], b[1] + 1)

        def prev(b):
            return (b[0], b[1] - 1)

        def index(b):
            return per_batch(b, 1, 0)

        def jobs(b, before, more, first, ahead, steady):
            base = per_batch(b, len(steady), 2 * len(first) - len(steady)) if before else len(first)
            names = [n for n in steady if (before if n not in ahead else more)]
            return {n: base + k for k, n in enumerate(names)}

        PROJECT_A, STEADY_A = ["q", "v"], ["q", "turn", "v", "out"]
        PROJECT_B, STEADY_B = ["x", "q", "k", "m", "v", "n"], ["turn", "x", "q", "k", "m", "v", "n", "out"]
        END_A = {"turn": 4 * B - 2, "out": 4 * B - 1}
        END_B = {"turn": 8 * B - 2, "out": 8 * B - 1}
        FIRST_A, FIRST_B = ({n: k for k, n in enumerate(p)} for p in (PROJECT_A, PROJECT_B))

        def jobs_a(b, before, more):
            return jobs(b, before, more, PROJECT_A, PROJECT_A, STEADY_A)

        def jobs_b(b, before, more):
            return jobs(b, before, more, PROJECT_B, PROJECT_B, STEADY_B)

        @block.sync
        def _(e):
            x_d = a["x"].rearrange("b (k p) t -> b p k t", p=P)

            def at_batch(n):
                return n if isinstance(n, int) else e.snap(n)

            def load_x(n, par):
                e.dma_start(xb[par], x_d[bass.ds(n, 1)].rearrange("o p k t -> (o p) k t")).then_inc(A["x_in"][par], 16)

            def load_mask(n, par):
                e.dma_start(crow[par], a["cond"][bass.ds(n, 1), :].rearrange("o t -> (o t)").partition_broadcast(P)).then_inc(A["mask_in"][par], 16)
                e.dma_start(mask_col[par][:, :], a["cond_cols"][bass.ds(n, 1)].rearrange("o p k -> (o p) k")).then_inc(A["mask_in"][par], 16)

            load_x(0, 0)
            e.dma_start(wq, a["wq_t"].rearrange("(k p) n -> p k n", p=P)).then_inc(A["weights_in"], 16)
            load_mask(0, 0)
            load_x(1, 1)
            load_mask(1, 1)
            e.dma_start(wo, a["wo_t"].rearrange("(k p) n -> p k n", p=P)).then_inc(A["weights_in"], 16)
            e.dma_start(cond_t[:, :], a["cond_t"]).then_inc(Bs["emb_in"], 16)
            e.dma_start(w_emb, a["w_emb"].rearrange("(k p) n -> p k n", p=P)).then_inc(Bs["emb_in"], 16)
            for dst, src in ((b_emb, "b_emb"), (g_norm, "g_norm"), (bias2, "bias2"), (b_ih, "b_ih"), (b_hh, "b_hh")):
                e.dma_start(dst[:, :], a[src]).then_inc(Bs["emb_in"], 16)
            for dst, src in ((g_q, "g_q"), (g_k, "g_k")):
                for j in range(4):
                    e.dma_start(dst[j * DH:(j + 1) * DH, :], a[src].rearrange("(p o) -> p o", o=1)).then_inc(Bs["emb_in"], 16)

            def pack_a(b):
                e.wait_ge(A["k_masked"], per_batch(b, 2, 2))
                pack(e, CA, b, qk_a[parity(b)], parts_a, HEADS_A)

            def store_x1(b):
                n = at_batch(index(b))
                e.wait_ge(A["added"], per_batch(b, 2, 2))
                e.dma_start(a["x1"][bass.ds(n, 1)].rearrange("o p n -> (o p) n"), xres.rearrange("p k t -> p (k t)")).then_inc(A["res_used"], 16)

            def slot_a(b, before, more, more2):
                par = parity(b)
                n, n2, unit = at_batch(index(b)), at_batch(index(b) + 2), at_batch(index(b) * UNIT)
                e.wait_ge(A["split_done"], per_batch(b, 1, 1))
                e.dma_start(stage[par], a["wall"][:, bass.ds(unit, UNIT)]).then_inc(A["stage_in"][par], 16)
                if more2:
                    e.wait_ge(A["v_ready"], per_batch(b, 4, 4))
                    load_x(n2, par)
                    e.wait_ge(A["bias_ready"], per_batch(b, 1, 1))
                    load_mask(n2, par)
                if more:
                    pack_a(nxt(b))
                if before:
                    store_x1(prev(b))
                e.wait_ge(A["res_used"], per_batch(b, 18, 18))
                e.dma_start(xres, x_d[bass.ds(n, 1)].rearrange("o p k t -> (o p) k t")).then_inc(A["res_in"], 16)
                if more:
                    CA.move_shift(e, nxt(b), parity(nxt(b)))

            def queue_slots(slot):
                slot((0, 0), False, True, True)
                with e.Fori(0, B // 2 - 2) as i:
                    slot((i, 1), True, True, True)
                    slot((i, 2), True, True, True)
                slot((B // 2 - 2, 1), True, True, True)
                slot((B // 2 - 2, 2), True, True, False)
                slot((B // 2 - 1, 1), True, False, False)

            pack_a((0, 0))
            CA.move_shift(e, (0, 0), 0)
            queue_slots(slot_a)
            store_x1((B // 2 - 1, 1))

            e.wait_ge(A["res_used"], 18 * B + 18)
            e.dma_start(wqkv, a["w_qkv"].rearrange("(k p) n -> p k n", p=P)).then_inc(Bs["weights_in"], 16)

            def load_x1(n):
                e.dma_start(x1, a["x1"][bass.ds(n, 1)].rearrange("o p (k t) -> (o p) k t", k=2)).then_inc(Bs["x1_in"], 16)

            load_x1(0)
            e.dma_start(wout, a["w_out"].rearrange("(k p) n -> p k n", p=P)).then_inc(Bs["weights_in"], 16)

            def pack_b(b):
                e.wait_ge(Bs["lo_ready"], per_batch(b, 4, 4))
                pack(e, CB_, b, qk_b[parity(b)], parts_b, HEADS_B)

            def slot_b(b, before, more, more2):
                n, n2 = at_batch(index(b)), at_batch(index(b) + 2)
                if more2:
                    e.wait_ge(Bs["xs_ready"], per_batch(b, 2, 4))
                    load_x1(n2)
                if more:
                    pack_b(nxt(b))
                if before:
                    e.wait_ge(Bs["x_written"], per_batch(b, 4, 0))
                e.dma_start(x1_res, a["x1"][bass.ds(n, 1)].rearrange("o p (k t) -> (o p) k t", k=2)).then_inc(Bs["res_in"], 16)
                if more:
                    CB_.move_shift(e, nxt(b), parity(nxt(b)))

            e.wait_ge(Bs["xs_ready"], 2)
            load_x1(1)
            pack_b((0, 0))
            CB_.move_shift(e, (0, 0), 0)
            queue_slots(slot_b)
            e.wait_ge(Bs["v_ready"], 2 * B)
            e.wait_ge(Bs["raw_ready"], 4 * B)
            e.dma_start(wqkv, a["w_ih"].rearrange("(k p) n -> p k n", p=P)).then_inc(Bs["wih_in"], 16)
            R["sync"](e)

        @block.tensor
        def _(e):
            pj = psum[0:2]

            def pj_wait(S, bank, job):
                wait_pos(e, S[f"pj{bank}_free"], job)

            def project_q(b, j):
                e.wait_ge(A["x_in"][parity(b)], loads(b))
                for g in range(2):
                    pj_wait(A, g, j)
                    for k in range(2):
                        mm = e.matmul(pj[g][:, :], wq[:, k, g * P:(g + 1) * P], xb[parity(b)][:, k, :], start=k == 0, stop=k == 1)
                    mm.then_inc(A[f"pj{g}_done"], 1)

            def project_v(b, j):
                for g in range(2):
                    pj_wait(A, g, j)
                    for y in range(2):
                        t = 2 * g + y
                        for k in range(2):
                            mm = e.matmul(pj[g][:, y * DIM_A:(y + 1) * DIM_A], xb[parity(b)][:, k, t * P:(t + 1) * P], wq[:, k, :],
                                          start=k == 0, stop=k == 1)
                    mm.then_inc(A[f"pj{g}_done"], 1)

            def turn_a(b, j):
                flat_heads = heads_a.rearrange("p t h d -> p t (h d)")
                for g in range(2):
                    e.wait_ge(CA.sems["pair_free"], per_batch(b, CA.pairs, 2 * g + 2 + CA.FREE0))
                    pj_wait(A, g, j)
                    for t in range(4):
                        mm = e.transpose(pj[g][:, t * P:(t + 1) * P], flat_heads[:, t, g * P:(g + 1) * P], ident[:, :])
                    mm.then_inc(A[f"pj{g}_done"], 1)

            def out_a(b, j):
                e.wait_ge(A["blended"], per_batch(b, 2, 2))
                for n in range(2):
                    pj_wait(A, n, j)
                    for g in range(2):
                        mm = e.matmul(pj[n][:, :], wo[:, g, n * P:(n + 1) * P], ctx_a[:, g, :], start=g == 0, stop=g == 1)
                    mm.then_inc(A[f"pj{n}_done"], 1)

            def attend(core, b, more, output):
                for x in range(core.tiles + core.LAG):
                    if x < core.tiles:
                        core.weight_tile(e, b, parity(b), x)
                    if x >= core.LAG:
                        core.pv_tile(e, b, parity(b), x - core.LAG)
                    if x == OUT_AT and output:
                        output()
                    if more and x < core.tiles:
                        for j in core.after[x]:
                            core.score_tile(e, nxt(b), parity(nxt(b)), j)
                if more:
                    core.max_rows(e, nxt(b))

            def first_scores(core):
                for j in range(core.tiles):
                    core.score_tile(e, (0, 0), 0, j)
                core.max_rows(e, (0, 0))

            e.wait_ge(A["weights_in"], 32)
            e.wait_ge(A["start_ready"], 10)
            e.wait_ge(A["ident_ready"], 5)
            project_q((0, 0), FIRST_A["q"])
            project_v((0, 0), FIRST_A["v"])
            e.wait_ge(Bs["emb_in"], 16 * 15)
            emb = psum[6]
            for n in range(2 * C):
                for k in range(C):
                    mm = e.matmul(emb[:, n * B:(n + 1) * B], w_emb[:, k, n * P:(n + 1) * P], cond_t[:, k * B:(k + 1) * B], start=k == 0, stop=k == C - 1)
            mm.then_inc(Bs["emb_done"], 1)
            first_scores(CA)
            e.wait_ge(Bs["mod_ready"], 2)

            def slot_a(e, b, before, more):
                J = jobs_a(b, before, more)
                if more:
                    project_q(nxt(b), J["q"])
                if before:
                    turn_a(prev(b), J["turn"])
                if more:
                    project_v(nxt(b), J["v"])
                attend(CA, b, more, before and (lambda: out_a(prev(b), J["out"])))

            slots(e, slot_a)
            turn_a((B // 2 - 1, 1), END_A["turn"])
            out_a((B // 2 - 1, 1), END_A["out"])

            e.wait_ge(Bs["start_ready"], 1)

            def project_b(b, J):
                e.wait_ge(Bs["xs_ready"], per_batch(b, 2, 2))
                for g in range(2):
                    pj_wait(Bs, g, J["x"])
                    for y in range(2):
                        f = 2 * g + y
                        for t in range(2):
                            mm = e.transpose(pj[g][:, y * SEQ_B + t * P:y * SEQ_B + (t + 1) * P], xs[:, t, f * P:(f + 1) * P], ident[:, :])
                    mm.then_inc(Bs[f"pj{g}_done"], 1)
                e.wait_ge(Bs["xn_ready"], per_batch(b, 4, 4))
                e.wait_ge(Bs["weights_in"], 32)
                for y in range(4):
                    pj_wait(Bs, y % 2, J["qk"[y // 2]])
                    for z in range(2):
                        o = 2 * y + z
                        for k in range(C):
                            mm = e.matmul(pj[y % 2][:, z * SEQ_B:(z + 1) * SEQ_B], wqkv[:, k, o * P:(o + 1) * P], xnT[:, k, :],
                                          start=k == 0, stop=k == C - 1)
                    mm.then_inc(Bs[f"pj{y % 2}_done"], 1)
                for y in range(2):
                    mean_squares(b, y, J)
                for t in range(2):
                    pj_wait(Bs, t, J["v"])
                    for k in range(C):
                        mm = e.matmul(pj[t][:, :], xnT[:, k, t * P:(t + 1) * P], wqkv[:, k, 2 * D:3 * D], start=k == 0, stop=k == C - 1)
                    mm.then_inc(Bs[f"pj{t}_done"], 1)
                for y in range(2, 4):
                    mean_squares(b, y, J)

            def mean_squares(b, y, J):
                pj_wait(Bs, y % 2, J["mn"[y // 2]])
                e.wait_ge(Bs["sq_ready"], per_batch(b, 4, y + 1))
                e.matmul(pj[y % 2][:, :], head_ones[:, :], sq[:, y, :], start=True, stop=True).then_inc(Bs[f"pj{y % 2}_done"], 1)

            def turn_b(b, j):
                flat_heads = heads_b.rearrange("p t h d -> p t (h d)")
                e.wait_ge(CB_.sems["pair_free"], per_batch(b, CB_.pairs, CB_.pairs + CB_.FREE0))
                for g in range(2):
                    pj_wait(Bs, g, j)
                    for z in range(2):
                        c = 2 * g + z
                        for t in range(2):
                            mm = e.transpose(pj[g][:, z * SEQ_B + t * P:z * SEQ_B + (t + 1) * P], flat_heads[:, t, c * P:(c + 1) * P], ident[:, :])
                    mm.then_inc(Bs[f"pj{g}_done"], 1)

            def out_b(b, j):
                e.wait_ge(Bs["turned"], per_batch(b, 2, 2))
                e.wait_ge(Bs["res_in"], per_batch(b, 16, 16))
                for g in range(2):
                    pj_wait(Bs, g, j)
                    for z in range(2):
                        c = 2 * g + z
                        for k in range(C):
                            e.matmul(pj[g][:, z * SEQ_B:(z + 1) * SEQ_B], wout[:, k, c * P:(c + 1) * P], ctx_b[:, k, :],
                                     start=k == 0, stop=False)
                        for t in range(2):
                            mm = e.matmul(pj[g][:, z * SEQ_B + t * P:z * SEQ_B + (t + 1) * P], x1_res[:, t, c * P:(c + 1) * P], ident[:, :],
                                          start=False, stop=t == 1)
                    mm.then_inc(Bs[f"pj{g}_done"], 1)

            project_b((0, 0), FIRST_B)
            first_scores(CB_)

            def slot_b(e, b, before, more):
                J = jobs_b(b, before, more)
                if before:
                    turn_b(prev(b), J["turn"])
                if more:
                    project_b(nxt(b), J)
                attend(CB_, b, more, before and (lambda: out_b(prev(b), J["out"])))

            slots(e, slot_b)
            turn_b((B // 2 - 1, 1), END_B["turn"])
            out_b((B // 2 - 1, 1), END_B["out"])
            e.wait_ge(R["S"]["init_done"], 2)
            e.wait_ge(Bs["wih_done"], 1)
            R["tensor"](e)

        @block.scalar
        def _(e):
            pj = psum[0:2]

            def high_a(b, j):
                for g in range(2):
                    e.wait_ge(A[f"pj{g}_done"], j + 1)
                    wait_pos(e, CA.sems["packed"], per_batch(b, 16 * 24, 0))
                    e.activation(parts_a[0][:, g, :], pj[g][:, :], ACT.Identity, accum_out=v_sum[:, bass.ds(index(b) * 2 + g, 1)]).then_inc(A["q_hi_ready"], 1)

            def values_a(b, j):
                for g in range(2):
                    e.wait_ge(A[f"pj{g}_done"], j + 1)
                    for y in range(2):
                        e.activation(v_a[parity(b)][:, 2 * g + y, :, 0:DH], pj[g][:, y * DIM_A:(y + 1) * DIM_A].rearrange("p (h d) -> p h d", d=DH),
                                     ACT.Copy).then_inc(A["v_ready"], 1)
                    e.wait_ge(A["v_ready"], per_batch(b, 4, 2 * g + 2))
                    e.nop().then_inc(A[f"pj{g}_free"], 1)

            def squares_a(b):
                for k in range(2):
                    e.wait_ge(A["added"], per_batch(b, 2, k + 1))
                    e.activation(squares[k], xres[:, k, :], ACT.Square, accum_out=ssq[:, bass.ds(index(b) * 2 + k, 1)]).then_inc(A["res_used"], 1)

            def slot_a(e, b, before, more):
                J = jobs_a(b, before, more)
                if more:
                    high_a(nxt(b), J["q"])
                    values_a(nxt(b), J["v"])
                e.wait_ge(A["bias_ready"], per_batch(b, 1, 1))
                for x in range(CA.tiles):
                    if x == ADD_AT + 3 and before:
                        squares_a(prev(b))
                    CA.exp_tile(e, b, x, parity(b))
                if more:
                    CA.shift_rows(e, nxt(b))

            high_a((0, 0), FIRST_A["q"])
            values_a((0, 0), FIRST_A["v"])
            CA.shift_rows(e, (0, 0))
            slots(e, slot_a)
            squares_a((B // 2 - 1, 1))

            e.wait_ge(A["res_used"], 18 * B + 18)
            e.activation(rstd[:, :], ssq[:, :], ACT.Sqrt, scale=1 / D, bias=eps[:, :]).then_inc(Bs["rstd0"], 1)
            e.wait_ge(Bs["start_ready"], 1)

            def project_b(b, J):
                par = parity(b)
                e.wait_ge(Bs["modb_ready"], per_batch(b, 1, 1))
                for g in range(2):
                    e.wait_ge(Bs[f"pj{g}_done"], J["x"] + 1)
                    for y in range(2):
                        f = 2 * g + y
                        ins = e.activation(xnT[:, f, :], pj[g][:, y * SEQ_B:(y + 1) * SEQ_B], ACT.Identity,
                                           scale=mod_b[par][:, f:f + 1], bias=mod_b[par][:, C + f:C + f + 1])
                        ins.then_inc(Bs["xn_ready"], 1)
                    e.wait_ge(Bs["xn_ready"], per_batch(b, 4, 2 * g + 2))
                    e.nop().then_inc(Bs[f"pj{g}_free"], 1)
                for y in range(4):
                    e.wait_ge(Bs[f"pj{y % 2}_done"], J["qk"[y // 2]] + 1)
                    wait_pos(e, Bs["lo_ready"], per_batch(b, 4, 0))
                    e.activation(raw[:, 2 * y:2 * y + 2, :].rearrange("p a n -> p (a n)"), pj[y % 2][:, :], ACT.Copy).then_inc(Bs["raw_ready"], 1)
                    e.activation(sq[:, y, :], pj[y % 2][:, :], ACT.Square).then_inc(Bs["sq_ready"], 1)
                    e.wait_ge(Bs["raw_ready"], per_batch(b, 4, y + 1))
                    e.wait_ge(Bs["sq_ready"], per_batch(b, 4, y + 1))
                    e.nop().then_inc(Bs[f"pj{y % 2}_free"], 1)
                for y in range(2):
                    root(b, y, J)
                for t in range(2):
                    e.wait_ge(Bs[f"pj{t}_done"], J["v"] + 1)
                    e.activation(v_b[par][:, t, :, 0:DH], pj[t][:, :].rearrange("p (h d) -> p h d", d=DH), ACT.Copy).then_inc(Bs["v_ready"], 1)
                    e.wait_ge(Bs["v_ready"], per_batch(b, 2, t + 1))
                    e.nop().then_inc(Bs[f"pj{t}_free"], 1)
                for y in range(2, 4):
                    root(b, y, J)

            def root(b, y, J):
                e.wait_ge(Bs[f"pj{y % 2}_done"], J["mn"[y // 2]] + 1)
                e.activation(sq[:, y, :], pj[y % 2][:, :], ACT.Sqrt, bias=eps[:, :]).then_inc(Bs["root_ready"], 1)
                e.wait_ge(Bs["root_ready"], per_batch(b, 4, y + 1))
                e.nop().then_inc(Bs[f"pj{y % 2}_free"], 1)

            def turned_b(b, j):
                for g in range(2):
                    e.wait_ge(Bs[f"pj{g}_done"], j + 1)
                    wait_pos(e, Bs["x_written"], per_batch(b, 4, 0))
                    e.activation(ctx_b[:, 2 * g:2 * g + 2, :].rearrange("p z n -> p (z n)"), pj[g][:, :], ACT.Copy).then_inc(Bs["turned"], 1)
                    e.wait_ge(Bs["turned"], per_batch(b, 2, g + 1))
                    e.nop().then_inc(Bs[f"pj{g}_free"], 1)

            def slot_b(e, b, before, more):
                J = jobs_b(b, before, more)
                if before:
                    turned_b(prev(b), J["turn"])
                if more:
                    project_b(nxt(b), J)
                for x in range(CB_.tiles):
                    CB_.exp_tile(e, b, x, parity(b))
                if more:
                    CB_.shift_rows(e, nxt(b))

            project_b((0, 0), FIRST_B)
            CB_.shift_rows(e, (0, 0))
            slots(e, slot_b)
            turned_b((B // 2 - 1, 1), END_B["turn"])

            e.wait_ge(Bs["wih_in"], 16)
            e.activation(wih_parts[0].rearrange("p k n -> p (k n)"), wqkv.rearrange("p k n -> p (k n)"), ACT.Copy, scale=SC).then_inc(Bs["wih_hi"], 1)
            e.wait_ge(Bs["x_written"], 4 * B)
            e.wait_ge(R["S"]["init_done"], 2)
            R["scalar"](e)

        @block.vector
        def _(e):
            pj = psum[0:2]
            e.memset(head_ones[:, :], 0.0).then_inc(A["start_ready"], 1)
            e.wait_ge(A["start_ready"], 1)
            for j in range(4):
                e.memset(head_ones[j * DH:(j + 1) * DH, j * DH:(j + 1) * DH], 1.0 / DH).then_inc(A["start_ready"], 1)
            for k in range(2):
                e.memset(v_a[k][:, :, :, DH:VW], 1.0).then_inc(A["start_ready"], 1)
                e.memset(qk_a[k][1][ROWS:ROWS + 1, :, :], MAX_SCALE).then_inc(A["start_ready"], 1)
            e.memset(eps[:, :], 1e-6).then_inc(A["start_ready"], 1)

            def low_a(b):
                for g in range(2):
                    e.wait_ge(A["q_hi_ready"], per_batch(b, 2, g + 1))
                    e.tensor_tensor(parts_a[1][:, g, :], pj[g][:, :], parts_a[0][:, g, :], ALU.subtract).then_inc(A["q_lo_ready"], 1)
                    e.wait_ge(A["q_lo_ready"], per_batch(b, 2, g + 1))
                    e.nop().then_inc(A[f"pj{g}_free"], 1)

            def attend(core, b, more, add):
                for x in range(core.tiles + core.LAG):
                    if x >= core.LAG:
                        y = x - core.LAG
                        per_pair = core.tiles // core.pairs
                        if y % per_pair == per_pair - 1:
                            core.divide(e, b, y // per_pair)
                    if x == ADD_AT and add:
                        add()
                    if more and x < core.tiles:
                        for j in core.after[x]:
                            core.max_tile(e, nxt(b), j)

            def blend_a(b, j):
                e.wait_ge(A["row_scaled"], per_batch(b, 1, 1))
                for g in range(2):
                    e.wait_ge(A[f"pj{g}_done"], j + 1)
                    e.scalar_tensor_tensor(out=ctx_a[:, g, :], in0=irow[parity(b)], scalar=v_sum[:, bass.ds(index(b) * 2 + g, 1)],
                                           in1=pj[g][:, :], op0=ALU.mult, op1=ALU.add).then_inc(A["blended"], 1)
                    e.wait_ge(A["blended"], per_batch(b, 2, g + 1))
                    e.nop().then_inc(A[f"pj{g}_free"], 1)

            def add_a(b, j):
                e.wait_ge(A["res_in"], per_batch(b, 16, 16))
                for k in range(2):
                    e.wait_ge(A[f"pj{k}_done"], j + 1)
                    e.tensor_tensor(xres[:, k, :], pj[k][:, :], xres[:, k, :], ALU.add).then_inc(A["added"], 1)
                    e.wait_ge(A["added"], per_batch(b, 2, k + 1))
                    e.nop().then_inc(A[f"pj{k}_free"], 1)

            def slot_a(e, b, before, more):
                J = jobs_a(b, before, more)
                if more:
                    low_a(nxt(b))
                if before:
                    blend_a(prev(b), J["turn"])
                at = index(b) * UNIT
                e.wait_ge(A["stage_in"][parity(b)], loads(b))
                e.tensor_scalar(w_parts[0][:, bass.ds(at, UNIT)], stage[parity(b)], SC, None, ALU.mult).then_inc(A["split_hi"], 1)
                e.wait_ge(A["split_hi"], per_batch(b, 1, 1))
                e.scalar_tensor_tensor(out=w_parts[1][:, bass.ds(at, UNIT)], in0=stage[parity(b)], scalar=SC, in1=w_parts[0][:, bass.ds(at, UNIT)],
                                       op0=ALU.mult, op1=ALU.subtract).then_inc(A["split_done"], 1)
                attend(CA, b, more, before and (lambda: add_a(prev(b), J["out"])))

            low_a((0, 0))
            e.wait_ge(Bs["emb_done"], 1)
            emb = psum[6][:, 0:2 * C * B].rearrange("p (c b) -> p c b", b=B)
            e.tensor_tensor(mod[:, :, :], emb, b_emb[:, :].rearrange("p (c o) -> p c o", o=1).to_broadcast([P, 2 * C, B]), ALU.add).then_inc(Bs["mod_ready"], 1)
            e.wait_ge(Bs["mod_ready"], 1)
            e.tensor_scalar(mod[:, 0:C, :], mod[:, 0:C, :], 1.0, None, ALU.add).then_inc(Bs["mod0"], 1)
            e.wait_ge(Bs["mod0"], 1)
            e.tensor_tensor(mod[:, 0:C, :], mod[:, 0:C, :], g_norm[:, :].rearrange("p (c o) -> p c o", o=1).to_broadcast([P, C, B]), ALU.mult).then_inc(Bs["mod_ready"], 1)
            e.tensor_copy(b_gates[:, :], b_ih[:, :]).then_inc(Bs["mod0"], 1)
            e.wait_ge(Bs["mod0"], 2)
            e.tensor_tensor(b_gates[:, 0:2 * C], b_ih[:, 0:2 * C], b_hh[:, 0:2 * C], ALU.add)
            for j in range(CA.tiles):
                CA.max_tile(e, (0, 0), j)
            slots(e, slot_a)
            blend_a((B // 2 - 1, 1), END_A["turn"])
            add_a((B // 2 - 1, 1), END_A["out"])

            e.wait_ge(A["res_used"], 18 * B + 18)
            e.wait_ge(Bs["rstd0"], 1)
            e.reciprocal(rstd[:, :], rstd[:, :]).then_inc(Bs["rstd_ready"], 1)
            for k in range(2):
                e.memset(v_b[k][:, :, :, DH:VW], 1.0).then_inc(Bs["rstd_ready"], 1)
                e.memset(qk_b[k][1][ROWS:ROWS + 1, :, :], MAX_SCALE).then_inc(Bs["rstd_ready"], 1)
            e.wait_ge(Bs["rstd_ready"], 5)
            e.nop().then_inc(Bs["start_ready"], 1)

            def scaled(b):
                par = parity(b)
                e.wait_ge(Bs["x1_in"], per_batch(b, 16, 16))
                e.tensor_copy(mod_b[par][:, :].rearrange("p (c o) -> p c o", o=1), mod[:, :, bass.ds(index(b), 1)]).then_inc(Bs["modb_ready"], 1)
                wait_pos(e, Bs["xn_ready"], per_batch(b, 4, 0))
                for t in range(2):
                    e.tensor_scalar(xs[:, t, :], x1[:, t, :], rstd[:, bass.ds(index(b) * 2 + t, 1)], None, ALU.mult).then_inc(Bs["xs_ready"], 1)

            def normalise(b, y):
                e.wait_ge(Bs["root_ready"], per_batch(b, 4, y + 1))
                e.reciprocal(sq[:, y, :], sq[:, y, :]).then_inc(Bs["half_ready"], 1)
                e.wait_ge(Bs["half_ready"], per_batch(b, 4, y + 1))
                g = (g_q, g_k)[y // 2]
                flat2 = lambda v: v.rearrange("p a n -> p (a n)")
                src = flat2(raw[:, 2 * y:2 * y + 2, :])
                z = 2 * (y % 2)
                wait_pos(e, CB_.sems["packed"], per_batch(b, 16 * 24, 0))
                e.scalar_tensor_tensor(out=flat2(parts_b[2 * (y // 2)][:, z:z + 2, :]), in0=src, scalar=g[:, 0:1], in1=sq[:, y, :],
                                       op0=ALU.mult, op1=ALU.mult).then_inc(Bs["hi_ready"], 1)
                e.scalar_tensor_tensor(out=src, in0=src, scalar=g[:, 0:1], in1=sq[:, y, :],
                                       op0=ALU.mult, op1=ALU.mult).then_inc(Bs["norm_ready"], 1)

            def add_b(b, j):
                for c in range(C):
                    e.wait_ge(Bs[f"pj{c // 2}_done"], j + 1)
                    z = c % 2
                    e.tensor_tensor(X[:, c, 0:T * B].rearrange("p (t b) -> p t b", b=B)[:, :, bass.ds(index(b), 1)],
                                    pj[c // 2][:, z * SEQ_B:(z + 1) * SEQ_B].rearrange("p (t o) -> p t o", o=1),
                                    ctx_b[:, c, :].rearrange("p (t o) -> p t o", o=1), ALU.add).then_inc(Bs["x_written"], 1)
                    if z == 1:
                        e.wait_ge(Bs["x_written"], per_batch(b, 4, c + 1))
                        e.nop().then_inc(Bs[f"pj{c // 2}_free"], 1)

            def slot_b(e, b, before, more):
                J = jobs_b(b, before, more)
                if more:
                    scaled(nxt(b))
                    for y in range(4):
                        normalise(nxt(b), y)
                attend(CB_, b, more, before and (lambda: add_b(prev(b), J["out"])))

            scaled((0, 0))
            for y in range(4):
                normalise((0, 0), y)
            for j in range(CB_.tiles):
                CB_.max_tile(e, (0, 0), j)
            slots(e, slot_b)
            add_b((B // 2 - 1, 1), END_B["out"])

            e.wait_ge(Bs["wih_hi"], 1)
            e.scalar_tensor_tensor(out=wih_parts[1].rearrange("p k n -> p (k n)"), in0=wqkv.rearrange("p k n -> p (k n)"), scalar=SC,
                                   in1=wih_parts[0].rearrange("p k n -> p (k n)"), op0=ALU.mult, op1=ALU.subtract).then_inc(Bs["wih_done"], 1)
            R["vector_start"](e)
            R["vector"](e)

        @block.gpsimd
        def _(e):
            CA.prime(e)
            CB_.prime(e)
            e.nop().then_inc(A["split_done"], 2)
            e.nop().then_inc(A["res_used"], 18)
            e.memset(ident[:, :], 0.0).then_inc(A["ident_ready"], 1)
            e.wait_ge(A["ident_ready"], 1)
            e.affine_select(out=ident[:, :], in_=ident[:, :], compare_op=ALU.not_equal, fill=1.0, base=0,
                            pattern=[[-1, P]], channel_multiplier=1).then_inc(A["ident_ready"], 1)

            def masks(b):
                par = parity(b)
                e.wait_ge(A["mask_in"][par], loads(b) * 2)
                wait_pos(e, CA.sems["pv_done"], per_batch(b, CA.tiles, CA.PV0 - CA.tiles))
                for g in range(2):
                    e.wait_ge(A["q_hi_ready"], per_batch(b, 2, g + 1))
                    e.tensor_tensor(parts_a[2][:, g, :], parts_a[0][:, g, :], crow[par][:, :], ALU.mult)
                    e.wait_ge(A["q_lo_ready"], per_batch(b, 2, g + 1))
                    e.tensor_tensor(parts_a[3][:, g, :], parts_a[1][:, g, :], crow[par][:, :], ALU.mult).then_inc(A["k_masked"], 1)
                wait_pos(e, A["row_scaled"], per_batch(b, 1, 0))
                e.tensor_tensor(tmp_row[:, :], one_row[:, :], crow[par][:, :], ALU.subtract).then_inc(A["row_ready"], 1)
                wait_pos(e, A["blended"], per_batch(b, 2, -2))
                e.wait_ge(A["row_ready"], per_batch(b, 1, 1))
                e.tensor_tensor(irow[par][:, :], tmp_row[:, :], over_row[:, :], ALU.mult).then_inc(A["row_scaled"], 1)
                e.tensor_tensor(guard_col[par][:, :], one_row[:, 0:4], mask_col[par][:, :], ALU.subtract).then_inc(A["col_ready"], 1)
                e.tensor_tensor(keep_col[par][:, :], one_row[:, 0:4], mask_col[par][:, :], ALU.mult).then_inc(A["col_ready"], 1)
                e.wait_ge(A["col_ready"], per_batch(b, 2, 2))
                e.tensor_tensor(mask_bias[par][:, :], guard_col[par][:, :], big[:, :], ALU.mult).then_inc(A["bias_ready"], 1)

            one_row, _x = cut(ARENA - 1540, (SEQ_A,))
            over_row, _x = cut(ARENA - 1028, (SEQ_A,))
            tmp_row, _x = cut(ARENA - 516, (SEQ_A,))
            big, _x = cut(ARENA - 4, (4,))
            e.memset(one_row[:, :], 1.0).then_inc(A["ident_ready"], 1)
            e.memset(over_row[:, :], 1.0 / SEQ_A).then_inc(A["ident_ready"], 1)
            e.memset(big[:, :], NEG).then_inc(A["ident_ready"], 1)
            e.wait_ge(A["ident_ready"], 5)
            masks((0, 0))

            def slot_a(e, b, before, more):
                if more:
                    masks(nxt(b))

            slots(e, slot_a)

            def low_b(b):
                wait_pos(e, CB_.sems["pv_done"], per_batch(b, CB_.tiles, CB_.PV0 - CB_.tiles))
                for y in range(4):
                    e.wait_ge(Bs["norm_ready"], per_batch(b, 4, y + 1))
                    z = 2 * (y % 2)
                    e.tensor_tensor(parts_b[2 * (y // 2) + 1][:, z:z + 2, :], raw[:, 2 * y:2 * y + 2, :], parts_b[2 * (y // 2)][:, z:z + 2, :],
                                    ALU.subtract).then_inc(Bs["lo_ready"], 1)

            low_b((0, 0))

            def slot_b(e, b, before, more):
                if more:
                    low_b(nxt(b))

            slots(e, slot_b)
            e.wait_ge(Bs["x_written"], 4 * B)
            e.wait_ge(R["S"]["init_done"], 2)
            R["gpsimd"](e)


def kernel(x, cond_2048, L0_cond_Wq, L0_cond_Wo, L1_cond_W_emb, L1_cond_b_emb, L1_cond_g_norm, L1_cond_W_qkv, L1_cond_g_q, L1_cond_g_k,
           L1_cond_W_out, L2_cond_coupling, L2_cond_bias, L3_cond_W_ih, L3_cond_W_hh, L3_cond_b_ih, L3_cond_b_hh):
    import numpy as np
    import concourse.bacc as bacc
    from concourse.bass_utils import run_bass_kernel_spmd as launch

    flat = np.ascontiguousarray
    rows = lambda w: np.asarray(w).reshape(C, P, -1).transpose(1, 0, 2).reshape(P, -1)
    cols = lambda v: flat(np.asarray(v).reshape(-1, P).T)
    cond = np.asarray(cond_2048)
    arrays = dict(
        x=x, cond=cond,
        cond_t=flat(rows(cond.T)),
        cond_cols=flat(cond.reshape(B, C, P).transpose(0, 2, 1)),
        wq_t=flat(np.asarray(L0_cond_Wq).T), wo_t=flat(np.asarray(L0_cond_Wo).T),
        w_emb=L1_cond_W_emb, b_emb=cols(L1_cond_b_emb), g_norm=cols(L1_cond_g_norm), w_qkv=L1_cond_W_qkv, g_q=L1_cond_g_q, g_k=L1_cond_g_k,
        w_out=L1_cond_W_out, wall=flat(np.concatenate([rows(np.asarray(L2_cond_coupling).T), rows(L3_cond_W_hh)], axis=1)),
        bias2=cols(L2_cond_bias), w_ih=L3_cond_W_ih, b_ih=cols(L3_cond_b_ih), b_hh=cols(L3_cond_b_hh))
    arrays = {n: flat(v) for n, v in arrays.items()}
    nc = bacc.Bacc("TRN2", target_bir_lowering=False, num_devices=1)
    aps = {n: nc.dram_tensor("in_" + n, v.shape, F32, kind="ExternalInput").ap() for n, v in arrays.items()}
    aps["x1"] = nc.dram_tensor("x1_scratch", (B, P, 2 * SEQ_A), F32).ap()
    aps["out"] = nc.dram_tensor("out_y", (P, CHUNKS, C * CH * B), F32, kind="ExternalOutput").ap()
    build(nc, aps)
    got = launch(nc, [{"in_" + n: v for n, v in arrays.items()}], core_ids=[0]).results[0]["out_y"]
    return flat(np.asarray(got).reshape(P, CHUNKS, C, CH, B).transpose(4, 1, 3, 2, 0).reshape(B, T, D))
```
